# Optimizing a Trainium2 kernel written in Bass

```python
import numpy as np
import jax
import jax.numpy as jnp

def _softmax(x, axis=-1):
    return jax.nn.softmax(x, axis=axis)
def _gelu(x):
    return jax.nn.gelu(x, approximate=True)
def _silu(x):
    return jax.nn.silu(x)
def _sigmoid(x):
    return jax.nn.sigmoid(x)
def _layernorm(x, axis=-1, eps=1e-5):
    m = jnp.mean(x, axis=axis, keepdims=True)
    v = jnp.var(x, axis=axis, keepdims=True)
    return (x - m) / jnp.sqrt(v + eps)
def _scatter_add(tgt, idx, src, axis=0):
    return tgt.at[idx].add(src)
def _segment_sum(src, seg, n):
    return jax.ops.segment_sum(src, seg, n)

kernel_name = 'mk_conv_preact_d4_conv_nchw96_bbbf1d'

def setup_inputs(seed: int = 0):
    np.random.seed(seed)
    _w = jnp.asarray
    def _rec_inputs():
        import jax
        import jax.numpy as jnp
        _gk = jax.random.key(seed)
        x = -0.001174 + 1 * jax.random.normal(jax.random.fold_in(_gk, 1), (4, 96, 56, 56), jnp.float32)
        return x
    x = _rec_inputs()
    def _L0_conv_setup():
        import jax, jax.numpy as jnp
        import numpy as np
        NUM_HEADS = 3
        key = jax.random.key(seed)
        k1, k2, k3 = jax.random.split(key, 3)
        B, C, H, W = (4, 96, 56, 56)
        rd = C // 2
        x = jax.random.normal(k1, (B, C, H, W), dtype=jnp.float32)
        w_qkv = jax.random.normal(k2, (3 * rd, C), dtype=jnp.float32) * 0.02
        w_proj = jax.random.normal(k3, (C, rd), dtype=jnp.float32) * 0.02
        b_proj = jnp.zeros((C,), dtype=jnp.float32)
        return {'x': x, 'w_qkv': w_qkv, 'w_proj': w_proj, 'b_proj': b_proj}
    _L0_conv_all = _L0_conv_setup()
    _L0_conv_in = {k: v for k, v in _L0_conv_all.items() if k in ('w_qkv', 'w_proj', 'b_proj', )}
    del _L0_conv_all

    def _L1_conv_setup():
        import jax, jax.numpy as jnp
        from jax import lax
        import numpy as np
        B, DM, H, W = (2, 96, 64, 64)
        DI, K, N, R = (192, 8, 16, 6)
        C_PROJ = R + 2 * N

        def _diag_idx(h, w):
            return (jnp.arange(h)[:, None] + jnp.arange(w)[None, :]) % w

        def _adiag_idx(h, w):
            return (jnp.arange(w)[None, :] - jnp.arange(h)[:, None]) % w

        def _gather(x, idx):
            g = jnp.take_along_axis(x, idx[None, None], axis=3)
            return jnp.swapaxes(g, -1, -2).reshape(x.shape[0], x.shape[1], -1)

        def _scatter(flat, shape, inv_idx):
            b, c, h, w = shape
            t = jnp.swapaxes(flat.reshape(b, c, w, h), -1, -2)
            return jnp.take_along_axis(t, inv_idx[None, None], axis=3)

        def cross_scan(x):
            b, c, h, w = x.shape
            x0 = x.reshape(b, c, -1)
            x1 = jnp.swapaxes(x, 2, 3).reshape(b, c, -1)
            x4 = _gather(x, _diag_idx(h, w))
            x5 = _gather(x, _adiag_idx(h, w))
            return jnp.stack([x0, x1, x0[..., ::-1], x1[..., ::-1], x4, x5, x4[..., ::-1], x5[..., ::-1]], axis=1)

        def cross_merge(ys, h, w):
            b, k, d, L = ys.shape
            y02 = ys[:, 0:2] + ys[:, 2:4][..., ::-1]
            y_rb = y02[:, 0] + jnp.swapaxes(y02[:, 1].reshape(b, d, w, h), -1, -2).reshape(b, d, L)
            y46 = ys[:, 4:6] + ys[:, 6:8][..., ::-1]
            y_da = _scatter(y46[:, 0], (b, d, h, w), _adiag_idx(h, w)) + _scatter(y46[:, 1], (b, d, h, w), _diag_idx(h, w))
            return y_rb.reshape(b, d, h, w) + y_da

        def selective_scan(u, delta, A, Bs, Cs, Dv):

            def step(hc, inp):
                u_t, d_t, B_t, C_t = inp
                hc = hc * jnp.exp(d_t[..., None] * A[None]) + (d_t * u_t)[..., None] * B_t[:, :, None, :]
                return (hc, jnp.einsum('bkdn,bkn->bkd', hc, C_t))
            seq = (jnp.moveaxis(u, -1, 0), jnp.moveaxis(delta, -1, 0), jnp.moveaxis(Bs, -1, 0), jnp.moveaxis(Cs, -1, 0))
            h0 = jnp.zeros(u.shape[:3] + (A.shape[-1],), u.dtype)
            _, ys = lax.scan(step, h0, seq)
            return jnp.moveaxis(ys, 0, -1) + u * Dv[None, :, :, None]
        key = jax.random.key(seed)
        ks = jax.random.split(key, 9)
        return dict(x=jax.random.normal(ks[0], (B, DM, H, W), jnp.float32), w_in=jax.random.normal(ks[1], (2 * DI, DM), jnp.float32) * 0.05, conv_w=jax.random.normal(ks[2], (DI, 1, 3, 3), jnp.float32) * 0.1, conv_b=jax.random.normal(ks[3], (DI,), jnp.float32) * 0.02, x_proj_weight=jax.random.normal(ks[4], (K, C_PROJ, DI), jnp.float32) * 0.05, dt_projs_weight=jax.random.normal(ks[5], (K, DI, R), jnp.float32) * 0.1, dt_projs_bias=jax.random.normal(ks[6], (K, DI), jnp.float32) * 0.1, A_logs=jnp.log(jax.random.uniform(ks[7], (K * DI, N), jnp.float32, 1.0, 16.0)), Ds=jnp.ones((K * DI,), jnp.float32), ln_w=jnp.ones((DI,), jnp.float32), ln_b=jnp.zeros((DI,), jnp.float32), w_out=jax.random.normal(ks[8], (DM, DI), jnp.float32) * 0.05)
    _L1_conv_all = _L1_conv_setup()
    _L1_conv_in = {k: v for k, v in _L1_conv_all.items() if k in ('w_in', 'conv_w', 'conv_b', 'x_proj_weight', 'dt_projs_weight', 'dt_projs_bias', 'A_logs', 'Ds', 'ln_w', 'ln_b', 'w_out', )}
    del _L1_conv_all

    def _L2_conv_setup():
        import jax, jax.numpy as jnp
        import numpy as np
        K = 8
        LOCAL_WINDOW_RATIO = 0.25
        NEG = -1000000000.0
        LN_EPS = 1e-05
        NORM_EPS = 1e-12

        def _window_indices(H, W):
            lws = max(3, int(min(H, W) * LOCAL_WINDOW_RATIO))
            if lws % 2 == 0:
                lws += 1
            half = lws // 2
            off = jnp.arange(-half, half + 1)
            dy, dx = jnp.meshgrid(off, off, indexing='ij')
            dy = dy.reshape(-1)
            dx = dx.reshape(-1)
            py, px = jnp.meshgrid(jnp.arange(H), jnp.arange(W), indexing='ij')
            py = py.reshape(-1)
            px = px.reshape(-1)
            ny = py[:, None] + dy[None, :]
            nx = px[:, None] + dx[None, :]
            valid = (ny >= 0) & (ny < H) & (nx >= 0) & (nx < W)
            idx = jnp.clip(ny, 0, H - 1) * W + jnp.clip(nx, 0, W - 1)
            return (idx, valid)
        key = jax.random.key(seed)
        ks = jax.random.split(key, 5)
        B, C, H, W = (4, 96, 48, 48)
        return {'x': jax.random.normal(ks[0], (B, C, H, W), jnp.float32), 'w1': jax.random.normal(ks[1], (2 * C, C), jnp.float32) * 0.05, 'b1': jax.random.normal(ks[2], (2 * C,), jnp.float32) * 0.05, 'w2': jax.random.normal(ks[3], (C, 2 * C), jnp.float32) * 0.05, 'b2': jax.random.normal(ks[4], (C,), jnp.float32) * 0.05, 'ln_w': jnp.ones((C,), jnp.float32), 'ln_b': jnp.zeros((C,), jnp.float32)}
    _L2_conv_all = _L2_conv_setup()
    _L2_conv_in = {k: v for k, v in _L2_conv_all.items() if k in ('w1', 'b1', 'w2', 'b2', 'ln_w', 'ln_b', )}
    del _L2_conv_all

    def _L3_conv_setup():
        import jax, jax.numpy as jnp
        import numpy as np
        B, DM, H, W = (2, 96, 48, 48)
        E = 192
        R, N = (6, 16)

        def conv2d(x, w, b, groups=1, pad=0):
            out = jax.lax.conv_general_dilated(x, w, window_strides=(1, 1), padding=[(pad, pad), (pad, pad)], dimension_numbers=('NCHW', 'OIHW', 'NCHW'), feature_group_count=groups)
            return out + b[None, :, None, None]
        key = jax.random.key(seed)
        ks = jax.random.split(key, 24)
        f = lambda k, shape, s: jax.random.normal(k, shape, jnp.float32) * s
        inp = {'x': jax.random.normal(ks[0], (B, DM, H, W), jnp.float32), 'in_proj_w': f(ks[1], (2 * E, DM), 0.05), 'conv_w': f(ks[2], (E, 1, 3, 3), 0.2), 'conv_b': f(ks[3], (E,), 0.1), 'x_proj_w': f(ks[4], (4, R + 2 * N, E), 0.01), 'dt_proj_w': f(ks[5], (4, E, R), 0.01), 'dt_proj_b': jnp.full((4, E), -9.0) + f(ks[6], (4, E), 0.1), 'A_log': jnp.tile(jnp.log(jnp.arange(1, N + 1, dtype=jnp.float32))[None, None, :], (4, E, 1)), 'Ds': jnp.ones((4, E), jnp.float32), 'ln_g': jnp.ones(E, jnp.float32), 'ln_b': jnp.zeros(E, jnp.float32), 'c1_w': f(ks[7], (2 * E, E, 1, 1), 0.05), 'c1_b': jnp.zeros(2 * E), 'bn1_g': jnp.ones(2 * E), 'bn1_b': jnp.zeros(2 * E), 'bn1_m': jnp.zeros(2 * E), 'bn1_v': jnp.ones(2 * E), 'c2_w': f(ks[8], (2 * E, 1, 3, 3), 0.2), 'c2_b': jnp.zeros(2 * E), 'bn2_g': jnp.ones(2 * E), 'bn2_b': jnp.zeros(2 * E), 'bn2_m': jnp.zeros(2 * E), 'bn2_v': jnp.ones(2 * E), 'c3_w': f(ks[9], (E // 2, 2 * E, 1, 1), 0.05), 'c3_b': jnp.zeros(E // 2), 'se1_w': f(ks[10], (E // 4, E // 2), 0.1), 'se1_b': jnp.zeros(E // 4), 'se2_w': f(ks[11], (E // 2, E // 4), 0.1), 'se2_b': jnp.zeros(E // 2)}
        return inp
    _L3_conv_all = _L3_conv_setup()
    _L3_conv_in = {k: v for k, v in _L3_conv_all.items() if k in ('in_proj_w', 'conv_w', 'conv_b', 'x_proj_w', 'dt_proj_w', 'dt_proj_b', 'A_log', 'Ds', 'ln_g', 'ln_b', 'c1_w', 'c1_b', 'bn1_g', 'bn1_b', 'bn1_m', 'bn1_v', 'c2_w', 'c2_b', 'bn2_g', 'bn2_b', 'bn2_m', 'bn2_v', 'c3_w', 'c3_b', 'se1_w', 'se1_b', 'se2_w', 'se2_b', )}
    del _L3_conv_all

    return {
        "x": x,
        "L0_conv_w_qkv": _L0_conv_in["w_qkv"],
        "L0_conv_w_proj": _L0_conv_in["w_proj"],
        "L0_conv_b_proj": _L0_conv_in["b_proj"],
        "L1_conv_w_in": _L1_conv_in["w_in"],
        "L1_conv_conv_w": _L1_conv_in["conv_w"],
        "L1_conv_conv_b": _L1_conv_in["conv_b"],
        "L1_conv_x_proj_weight": _L1_conv_in["x_proj_weight"],
        "L1_conv_dt_projs_weight": _L1_conv_in["dt_projs_weight"],
        "L1_conv_dt_projs_bias": _L1_conv_in["dt_projs_bias"],
        "L1_conv_A_logs": _L1_conv_in["A_logs"],
        "L1_conv_Ds": _L1_conv_in["Ds"],
        "L1_conv_ln_w": _L1_conv_in["ln_w"],
        "L1_conv_ln_b": _L1_conv_in["ln_b"],
        "L1_conv_w_out": _L1_conv_in["w_out"],
        "L2_conv_w1": _L2_conv_in["w1"],
        "L2_conv_b1": _L2_conv_in["b1"],
        "L2_conv_w2": _L2_conv_in["w2"],
        "L2_conv_b2": _L2_conv_in["b2"],
        "L2_conv_ln_w": _L2_conv_in["ln_w"],
        "L2_conv_ln_b": _L2_conv_in["ln_b"],
        "L3_conv_in_proj_w": _L3_conv_in["in_proj_w"],
        "L3_conv_conv_w": _L3_conv_in["conv_w"],
        "L3_conv_conv_b": _L3_conv_in["conv_b"],
        "L3_conv_x_proj_w": _L3_conv_in["x_proj_w"],
        "L3_conv_dt_proj_w": _L3_conv_in["dt_proj_w"],
        "L3_conv_dt_proj_b": _L3_conv_in["dt_proj_b"],
        "L3_conv_A_log": _L3_conv_in["A_log"],
        "L3_conv_Ds": _L3_conv_in["Ds"],
        "L3_conv_ln_g": _L3_conv_in["ln_g"],
        "L3_conv_ln_b": _L3_conv_in["ln_b"],
        "L3_conv_c1_w": _L3_conv_in["c1_w"],
        "L3_conv_c1_b": _L3_conv_in["c1_b"],
        "L3_conv_bn1_g": _L3_conv_in["bn1_g"],
        "L3_conv_bn1_b": _L3_conv_in["bn1_b"],
        "L3_conv_bn1_m": _L3_conv_in["bn1_m"],
        "L3_conv_bn1_v": _L3_conv_in["bn1_v"],
        "L3_conv_c2_w": _L3_conv_in["c2_w"],
        "L3_conv_c2_b": _L3_conv_in["c2_b"],
        "L3_conv_bn2_g": _L3_conv_in["bn2_g"],
        "L3_conv_bn2_b": _L3_conv_in["bn2_b"],
        "L3_conv_bn2_m": _L3_conv_in["bn2_m"],
        "L3_conv_bn2_v": _L3_conv_in["bn2_v"],
        "L3_conv_c3_w": _L3_conv_in["c3_w"],
        "L3_conv_c3_b": _L3_conv_in["c3_b"],
        "L3_conv_se1_w": _L3_conv_in["se1_w"],
        "L3_conv_se1_b": _L3_conv_in["se1_b"],
        "L3_conv_se2_w": _L3_conv_in["se2_w"],
        "L3_conv_se2_b": _L3_conv_in["se2_b"],
    }

def reference(x, L0_conv_w_qkv, L0_conv_w_proj, L0_conv_b_proj, L1_conv_w_in, L1_conv_conv_w, L1_conv_conv_b, L1_conv_x_proj_weight, L1_conv_dt_projs_weight, L1_conv_dt_projs_bias, L1_conv_A_logs, L1_conv_Ds, L1_conv_ln_w, L1_conv_ln_b, L1_conv_w_out, L2_conv_w1, L2_conv_b1, L2_conv_w2, L2_conv_b2, L2_conv_ln_w, L2_conv_ln_b, L3_conv_in_proj_w, L3_conv_conv_w, L3_conv_conv_b, L3_conv_x_proj_w, L3_conv_dt_proj_w, L3_conv_dt_proj_b, L3_conv_A_log, L3_conv_Ds, L3_conv_ln_g, L3_conv_ln_b, L3_conv_c1_w, L3_conv_c1_b, L3_conv_bn1_g, L3_conv_bn1_b, L3_conv_bn1_m, L3_conv_bn1_v, L3_conv_c2_w, L3_conv_c2_b, L3_conv_bn2_g, L3_conv_bn2_b, L3_conv_bn2_m, L3_conv_bn2_v, L3_conv_c3_w, L3_conv_c3_b, L3_conv_se1_w, L3_conv_se1_b, L3_conv_se2_w, L3_conv_se2_b):
    import jax
    import jax.numpy as jnp
    def _L0_conv_ref(x, w_qkv, w_proj, b_proj):
        import jax, jax.numpy as jnp
        import numpy as np
        NUM_HEADS = 3
        B, C, H, W = x.shape
        N = H * W
        hd = C // NUM_HEADS // 2
        scale = C ** (-0.5)
        tokens = jnp.transpose(x, (0, 2, 3, 1)).reshape(B, N, C)
        qkv = tokens @ w_qkv.T
        qkv = qkv.reshape(B, N, 3, NUM_HEADS, hd).transpose(2, 0, 3, 1, 4)
        q, k, v = (qkv[0], qkv[1], qkv[2])
        attn = jnp.einsum('bhnd,bhmd->bhnm', q, k) * scale
        attn = jax.nn.softmax(attn, axis=-1)
        out = jnp.einsum('bhnm,bhmd->bhnd', attn, v)
        out = out.transpose(0, 2, 1, 3).reshape(B, N, C // 2)
        out = out @ w_proj.T + b_proj
        return jnp.transpose(out.reshape(B, H, W, C), (0, 3, 1, 2))

    def _L1_conv_ref(x, w_in, conv_w, conv_b, x_proj_weight, dt_projs_weight, dt_projs_bias, A_logs, Ds, ln_w, ln_b, w_out):
        import jax, jax.numpy as jnp
        from jax import lax
        import numpy as np
        B, DM, H, W = (2, 96, 64, 64)
        DI, K, N, R = (192, 8, 16, 6)
        C_PROJ = R + 2 * N

        def _diag_idx(h, w):
            return (jnp.arange(h)[:, None] + jnp.arange(w)[None, :]) % w

        def _adiag_idx(h, w):
            return (jnp.arange(w)[None, :] - jnp.arange(h)[:, None]) % w

        def _gather(x, idx):
            g = jnp.take_along_axis(x, idx[None, None], axis=3)
            return jnp.swapaxes(g, -1, -2).reshape(x.shape[0], x.shape[1], -1)

        def _scatter(flat, shape, inv_idx):
            b, c, h, w = shape
            t = jnp.swapaxes(flat.reshape(b, c, w, h), -1, -2)
            return jnp.take_along_axis(t, inv_idx[None, None], axis=3)

        def cross_scan(x):
            b, c, h, w = x.shape
            x0 = x.reshape(b, c, -1)
            x1 = jnp.swapaxes(x, 2, 3).reshape(b, c, -1)
            x4 = _gather(x, _diag_idx(h, w))
            x5 = _gather(x, _adiag_idx(h, w))
            return jnp.stack([x0, x1, x0[..., ::-1], x1[..., ::-1], x4, x5, x4[..., ::-1], x5[..., ::-1]], axis=1)

        def cross_merge(ys, h, w):
            b, k, d, L = ys.shape
            y02 = ys[:, 0:2] + ys[:, 2:4][..., ::-1]
            y_rb = y02[:, 0] + jnp.swapaxes(y02[:, 1].reshape(b, d, w, h), -1, -2).reshape(b, d, L)
            y46 = ys[:, 4:6] + ys[:, 6:8][..., ::-1]
            y_da = _scatter(y46[:, 0], (b, d, h, w), _adiag_idx(h, w)) + _scatter(y46[:, 1], (b, d, h, w), _diag_idx(h, w))
            return y_rb.reshape(b, d, h, w) + y_da

        def selective_scan(u, delta, A, Bs, Cs, Dv):

            def step(hc, inp):
                u_t, d_t, B_t, C_t = inp
                hc = hc * jnp.exp(d_t[..., None] * A[None]) + (d_t * u_t)[..., None] * B_t[:, :, None, :]
                return (hc, jnp.einsum('bkdn,bkn->bkd', hc, C_t))
            seq = (jnp.moveaxis(u, -1, 0), jnp.moveaxis(delta, -1, 0), jnp.moveaxis(Bs, -1, 0), jnp.moveaxis(Cs, -1, 0))
            h0 = jnp.zeros(u.shape[:3] + (A.shape[-1],), u.dtype)
            _, ys = lax.scan(step, h0, seq)
            return jnp.moveaxis(ys, 0, -1) + u * Dv[None, :, :, None]
        b, _, h, w = x.shape
        L = h * w
        xz = jnp.einsum('bchw,dc->bdhw', x, w_in)
        xc, z = jnp.split(xz, 2, axis=1)
        z = jax.nn.silu(z)
        xc = lax.conv_general_dilated(xc, conv_w, (1, 1), 'SAME', feature_group_count=DI, dimension_numbers=('NCHW', 'OIHW', 'NCHW'))
        xc = jax.nn.silu(xc + conv_b[None, :, None, None])
        xs = cross_scan(xc)
        x_dbl = jnp.einsum('bkdl,kcd->bkcl', xs, x_proj_weight)
        dts, Bmat, Cmat = jnp.split(x_dbl, [R, R + N], axis=2)
        dts = jnp.einsum('bkrl,kdr->bkdl', dts, dt_projs_weight)
        delta = jax.nn.softplus(dts + dt_projs_bias[None, :, :, None])
        A = -jnp.exp(A_logs).reshape(K, DI, N)
        Dv = Ds.reshape(K, DI)
        ys = selective_scan(xs, delta, A, Bmat, Cmat, Dv)
        y = cross_merge(ys, h, w).reshape(b, DI, L)
        y = jnp.swapaxes(y, 1, 2)
        mu = y.mean(-1, keepdims=True)
        var = jnp.mean((y - mu) ** 2, axis=-1, keepdims=True)
        y = (y - mu) / jnp.sqrt(var + 1e-05) * ln_w + ln_b
        y = y.reshape(b, h, w, DI) * jnp.transpose(z, (0, 2, 3, 1))
        return jnp.einsum('bhwd,od->bohw', y, w_out)

    def _L2_conv_ref(x, w1, b1, w2, b2, ln_w, ln_b):
        import jax, jax.numpy as jnp
        import numpy as np
        K = 8
        LOCAL_WINDOW_RATIO = 0.25
        NEG = -1000000000.0
        LN_EPS = 1e-05
        NORM_EPS = 1e-12

        def _window_indices(H, W):
            lws = max(3, int(min(H, W) * LOCAL_WINDOW_RATIO))
            if lws % 2 == 0:
                lws += 1
            half = lws // 2
            off = jnp.arange(-half, half + 1)
            dy, dx = jnp.meshgrid(off, off, indexing='ij')
            dy = dy.reshape(-1)
            dx = dx.reshape(-1)
            py, px = jnp.meshgrid(jnp.arange(H), jnp.arange(W), indexing='ij')
            py = py.reshape(-1)
            px = px.reshape(-1)
            ny = py[:, None] + dy[None, :]
            nx = px[:, None] + dx[None, :]
            valid = (ny >= 0) & (ny < H) & (nx >= 0) & (nx < W)
            idx = jnp.clip(ny, 0, H - 1) * W + jnp.clip(nx, 0, W - 1)
            return (idx, valid)
        B, C, H, W = x.shape
        HW = H * W
        idx_w, valid = _window_indices(H, W)
        x_flat = x.transpose(0, 2, 3, 1).reshape(B, HW, C)
        n = jnp.linalg.norm(x_flat, axis=-1, keepdims=True)
        x_n = x_flat / jnp.maximum(n, NORM_EPS)
        win_n = x_n[:, idx_w, :]
        sims = jnp.einsum('bpc,bpwc->bpw', x_n, win_n)
        sims = jnp.where(valid[None], sims, NEG)
        top_sim, top_idx = jax.lax.top_k(sims, K)
        wts = jax.nn.softmax(top_sim, axis=-1)
        idx_g = jnp.take_along_axis(jnp.broadcast_to(idx_w[None], sims.shape), top_idx, axis=-1)
        feats = x_flat[jnp.arange(B)[:, None, None], idx_g]
        agg = jnp.einsum('bpk,bpkc->bpc', wts, feats)
        mu = jnp.mean(x_flat, axis=-1, keepdims=True)
        var = jnp.var(x_flat, axis=-1, keepdims=True)
        x_ln = (x_flat - mu) / jnp.sqrt(var + LN_EPS) * ln_w + ln_b
        enhanced = agg + x_ln
        h = jax.nn.relu(jnp.einsum('bpc,dc->bpd', enhanced, w1) + b1)
        ffn = jnp.einsum('bpd,cd->bpc', h, w2) + b2
        out = enhanced + ffn
        return out.reshape(B, H, W, C).transpose(0, 3, 1, 2)

    def _L3_conv_ref(x, in_proj_w, conv_w, conv_b, x_proj_w, dt_proj_w, dt_proj_b, A_log, Ds, ln_g, ln_b, c1_w, c1_b, bn1_g, bn1_b, bn1_m, bn1_v, c2_w, c2_b, bn2_g, bn2_b, bn2_m, bn2_v, c3_w, c3_b, se1_w, se1_b, se2_w, se2_b):
        import jax, jax.numpy as jnp
        import numpy as np
        B, DM, H, W = (2, 96, 48, 48)
        E = 192
        R, N = (6, 16)

        def conv2d(x, w, b, groups=1, pad=0):
            out = jax.lax.conv_general_dilated(x, w, window_strides=(1, 1), padding=[(pad, pad), (pad, pad)], dimension_numbers=('NCHW', 'OIHW', 'NCHW'), feature_group_count=groups)
            return out + b[None, :, None, None]
        Bs, _, Hs, Ws = x.shape
        L = Hs * Ws
        xz = jnp.einsum('bchw,oc->bohw', x, in_proj_w)
        xi, z = jnp.split(xz, 2, axis=1)
        xi = jax.nn.silu(conv2d(xi, conv_w, conv_b, groups=E, pad=1))
        xf = xi.reshape(Bs, E, L)
        xt = jnp.swapaxes(xi, 2, 3).reshape(Bs, E, L)
        xs = jnp.stack([xf, xf[..., ::-1], xt, xt[..., ::-1]], axis=1)
        dbc = jnp.einsum('bkcl,krc->bkrl', xs, x_proj_w)
        dlt, b, c = (dbc[:, :, :R], dbc[:, :, R:R + N], dbc[:, :, R + N:])
        dlt = jnp.einsum('bkrl,kdr->bkdl', dlt, dt_proj_w) + dt_proj_b[None, :, :, None]
        dlt = jax.nn.softplus(dlt)
        dA = dlt[..., None] * A_log[None, :, :, None, :]
        phi = jnp.exp(-jnp.cumsum(dA, axis=3))
        dbx = dlt[..., None] * jnp.swapaxes(b, 2, 3)[:, :, None] * xs[..., None]
        h = phi * jnp.cumsum(dbx / (phi + 1e-12), axis=3)
        y = jnp.einsum('bkdln,bknl->bkdl', h, c) + Ds[None, :, :, None]
        y1 = y[:, 0]
        y2 = y[:, 1, :, ::-1]
        y3 = jnp.swapaxes(y[:, 2].reshape(Bs, E, Ws, Hs), 2, 3).reshape(Bs, E, L)
        y4 = jnp.swapaxes(y[:, 3, :, ::-1].reshape(Bs, E, Ws, Hs), 2, 3).reshape(Bs, E, L)
        ys = (y1 + y2 + y3 + y4).reshape(Bs, E, Hs, Ws)
        yn = jnp.moveaxis(ys, 1, -1)
        mu = yn.mean(-1, keepdims=True)
        var = yn.var(-1, keepdims=True)
        yn = (yn - mu) / jnp.sqrt(var + 1e-05) * ln_g + ln_b
        u = jnp.moveaxis(yn, -1, 1) * z

        def bn(t, g, bb, m, v):
            return (t - m[None, :, None, None]) / jnp.sqrt(v + 1e-05)[None, :, None, None] * g[None, :, None, None] + bb[None, :, None, None]
        t = jax.nn.relu(bn(conv2d(u, c1_w, c1_b), bn1_g, bn1_b, bn1_m, bn1_v))
        t = jax.nn.relu(bn(conv2d(t, c2_w, c2_b, groups=2 * E, pad=1), bn2_g, bn2_b, bn2_m, bn2_v))
        t = conv2d(t, c3_w, c3_b)
        s = t.mean((2, 3))
        s = jax.nn.relu(s @ se1_w.T + se1_b)
        s = jax.nn.sigmoid(s @ se2_w.T + se2_b)
        return t + t * s[:, :, None, None]

    def _gn(v, G=32, eps=1e-5):
        B_, C_, H_, W_ = v.shape
        g = v.reshape(B_, G, C_ // G, H_, W_)
        m = jnp.mean(g, axis=(2, 3, 4), keepdims=True)
        s = jnp.var(g, axis=(2, 3, 4), keepdims=True)
        return ((g - m) / jnp.sqrt(s + eps)).reshape(v.shape)

    def _ln_c(v, eps=1e-6):
        m = jnp.mean(v, axis=1, keepdims=True)
        s = jnp.var(v, axis=1, keepdims=True)
        return (v - m) / jnp.sqrt(s + eps)

    def _ln_t(v, eps=1e-5):
        m = jnp.mean(v, axis=-1, keepdims=True)
        s = jnp.var(v, axis=-1, keepdims=True)
        return (v - m) / jnp.sqrt(s + eps)

    def _to_tokens(v):
        B_, C_, H_, W_ = v.shape
        return v.reshape(B_, C_, H_ * W_).transpose(0, 2, 1)
    def _from_tokens(t, like):
        B_, C_, H_, W_ = like.shape
        return t.transpose(0, 2, 1).reshape(B_, C_, H_, W_)

    x = x + _L0_conv_ref(_gn(x), L0_conv_w_qkv, L0_conv_w_proj, L0_conv_b_proj)
    x = x + _L1_conv_ref(_gn(x), L1_conv_w_in, L1_conv_conv_w, L1_conv_conv_b, L1_conv_x_proj_weight, L1_conv_dt_projs_weight, L1_conv_dt_projs_bias, L1_conv_A_logs, L1_conv_Ds, L1_conv_ln_w, L1_conv_ln_b, L1_conv_w_out)
    x = x + _L2_conv_ref(_gn(x), L2_conv_w1, L2_conv_b1, L2_conv_w2, L2_conv_b2, L2_conv_ln_w, L2_conv_ln_b)
    x = x + _L3_conv_ref(_gn(x), L3_conv_in_proj_w, L3_conv_conv_w, L3_conv_conv_b, L3_conv_x_proj_w, L3_conv_dt_proj_w, L3_conv_dt_proj_b, L3_conv_A_log, L3_conv_Ds, L3_conv_ln_g, L3_conv_ln_b, L3_conv_c1_w, L3_conv_c1_b, L3_conv_bn1_g, L3_conv_bn1_b, L3_conv_bn1_m, L3_conv_bn1_v, L3_conv_c2_w, L3_conv_c2_b, L3_conv_bn2_g, L3_conv_bn2_b, L3_conv_bn2_m, L3_conv_bn2_v, L3_conv_c3_w, L3_conv_c3_b, L3_conv_se1_w, L3_conv_se1_b, L3_conv_se2_w, L3_conv_se2_b)
    return x


_drawn_inputs = setup_inputs


def setup_inputs(seed=0):
    import zlib

    import numpy as np

    out = dict(_drawn_inputs(seed))
    spreads = {'L0_conv_b_proj': (0.0, 0.1),
     'L1_conv_Ds': (1.0, 0.6),
     'L1_conv_ln_w': (1.0, 0.2),
     'L1_conv_ln_b': (0.0, 0.1),
     'L2_conv_ln_w': (1.0, 0.2),
     'L2_conv_ln_b': (0.0, 0.1),
     'L3_conv_Ds': (1.0, 0.2),
     'L3_conv_ln_g': (1.0, 0.6),
     'L3_conv_ln_b': (0.0, 0.8),
     'L3_conv_c1_b': (0.0, 0.295),
     'L3_conv_bn1_g': (1.0, 0.6),
     'L3_conv_bn1_b': (0.0, 0.375),
     'L3_conv_bn1_m': (0.0, 0.417),
     'L3_conv_bn1_v': (1.0, 0.6),
     'L3_conv_c2_b': (0.0, 0.1),
     'L3_conv_bn2_g': (1.0, 0.6),
     'L3_conv_bn2_b': (0.0, 0.1),
     'L3_conv_bn2_m': (0.0, 0.1),
     'L3_conv_bn2_v': (1.0, 0.6),
     'L3_conv_c3_b': (0.0, 0.1),
     'L3_conv_se1_b': (0.0, 0.8),
     'L3_conv_se2_b': (0.0, 0.8)}
    factors = {'L0_conv_w_qkv': 8.0,
     'L0_conv_w_proj': 8.0,
     'L1_conv_x_proj_weight': 8.0,
     'L1_conv_dt_projs_weight': 8.0,
     'L1_conv_dt_projs_bias': 8.0,
     'L1_conv_A_logs': 8.0,
     'L2_conv_b1': 5.362,
     'L2_conv_b2': 2.816,
     'L3_conv_conv_w': 8.0,
     'L3_conv_conv_b': 8.0,
     'L3_conv_x_proj_w': 8.0,
     'L3_conv_dt_proj_w': 8.0,
     'L3_conv_dt_proj_b': 8.0,
     'L3_conv_A_log': 8.0,
     'L3_conv_se1_w': 8.0,
     'L3_conv_se2_w': 8.0}
    for name, (base, spread) in spreads.items():
        noise = np.random.default_rng([zlib.crc32(name.encode()), seed]).standard_normal(out[name].shape)
        drawn = base * np.exp(spread * noise) if base else spread * noise
        out[name] = jnp.asarray(drawn.astype(out[name].dtype))
    for name, factor in factors.items():
        out[name] = (out[name] * factor).astype(out[name].dtype)
    return out
```

```python
from contextlib import ExitStack

import numpy as np

import concourse.bass as bass
from concourse import mybir

F32 = mybir.dt.float32
BF16 = mybir.dt.bfloat16
ALU = mybir.AluOpType
ACT = mybir.ActivationFunctionType
AX = mybir.AxisListType

H = W = 56
L = H * W
T = 448
NT = L // T
C = 96
NI = 4


class Token:

    def __init__(self, queue, place):
        self.queue, self.place, self.used = queue, place, False


class Landed:

    def __init__(self, slot, value):
        self.slot, self.value = slot, value


class Queue:

    def __init__(self, sem):
        self.sem, self.items, self.last, self.seen = sem, [], None, {}

    def wait(self, *tokens):
        for t in tokens:
            if t is None:
                continue
            if isinstance(t, (list, tuple)):
                self.wait(*t)
            elif isinstance(t, Landed):
                if self.seen.get(t.slot, 0) < t.value:
                    self.seen[t.slot] = t.value
                    self.items.append(("landed", t))
            elif self.seen.get(t.queue, -1) < t.place:
                self.seen[t.queue] = t.place
                t.used = True
                self.items.append(("wait", t))

    def __call__(self, fn, *tokens):
        self.wait(*tokens)
        self.last = Token(self, len(self.items))
        self.items.append(("do", fn, self.last))
        return self.last

    def number(self):
        n = 0
        for item in self.items:
            if item[0] == "do" and item[2].used:
                n += 1
                item[2].value = n

    def emit(self, eng):
        for item in self.items:
            if item[0] == "wait":
                eng.wait_ge(item[1].queue.sem, item[1].value)
            elif item[0] == "landed":
                eng.wait_ge(item[1].slot, item[1].value)
            else:
                done = item[1](eng)
                if item[2].used:
                    done.then_inc(self.sem, 1)


class Program:

    NSLOT = 40

    def __init__(self, nc, ctx):
        self.nc = nc
        self.names = 0
        self.pe, self.act, self.dve, self.pool, self.sp = (
            Queue(ctx.enter_context(nc.semaphore(f"s_{n}"))) for n in ("pe", "act", "dve", "pool", "sp"))
        self.slots = [ctx.enter_context(nc.semaphore(f"s_dma{i}")) for i in range(self.NSLOT)]
        self.landed = [None] * self.NSLOT
        self.ndma = 0
        self.PS = ctx.enter_context(nc.psum_tensor("PS", [128, 8, 512], F32))

    def sb(self, ctx, name, shape, dt=F32):
        self.names += 1
        return ctx.enter_context(self.nc.sbuf_tensor(f"{name}_{self.names}", shape, dt))

    def dma(self, out, in_, *tokens):
        i = self.ndma % self.NSLOT
        self.ndma += 1
        self.sp.wait(self.landed[i])
        slot = self.slots[i]
        self.sp.wait(*tokens)
        self.sp.items.append(("do", lambda e: e.dma_start(out, in_).then_inc(slot, 16), Token(self.sp, len(self.sp.items))))
        self.landed[i] = Landed(slot, (self.landed[i].value if self.landed[i] else 0) + 16)
        return self.landed[i]

    def barrier(self):
        ends = [q.last for q in (self.pe, self.act, self.dve, self.pool)] + list(self.landed)
        for q in (self.pe, self.act, self.dve, self.pool, self.sp):
            q.wait(*[t for t in ends if not (isinstance(t, Token) and t.queue is q)])
        for q in (self.pe, self.act, self.dve, self.pool):
            q.wait(q.last)

    def emit(self):
        self.sp.wait(*self.landed)
        queues = (self.pe, self.act, self.dve, self.pool, self.sp)
        for q in queues:
            q.number()
        with self.nc.Block() as block:
            block.tensor(self.pe.emit)
            block.scalar(self.act.emit)
            block.vector(self.dve.emit)
            block.gpsimd(self.pool.emit)
            block.sync(self.sp.emit)


def view(t, off, dims, parts=None):
    base = t[:] if not isinstance(t, bass.AP) else t
    p = list(base.ap[0])
    if parts is not None:
        p[1] = parts
    return bass.AP(base.tensor, base.offset + off, [p] + [list(d) for d in dims])


def mm(out, lhsT, rhs, start=True, stop=True):
    return lambda e: e.matmul(out, lhsT, rhs, start=start, stop=stop)


def act(out, in_, fn, **kw):
    return lambda e: e.activation(out, in_, fn, **kw)


def tt(out, a, b, op):
    return lambda e: e.tensor_tensor(out, a, b, op)


def ts(out, a, s1, s2, op0, op1=ALU.bypass):
    if s2 is None:
        return lambda e: e.tensor_scalar(out, a, s1, None, op0)
    return lambda e: e.tensor_scalar(out, a, s1, s2, op0, op1)


def stt(out, a, s, b, op0, op1, **kw):
    return lambda e: e.scalar_tensor_tensor(out=out, in0=a, scalar=s, in1=b, op0=op0, op1=op1, **kw)


def copy(out, a):
    return lambda e: e.tensor_copy(out, a)


def groupnorm(P, K, g, x, bank, ready, scratch, small):
    s, m, v, r = (small[0:C, i:i + 1] for i in range(4))
    pm = P.PS[0:C, bank, 0:1]
    a = P.dve(lambda e: e.reduce_sum(s, x, axis=AX.X), ready)
    a = P.pe(mm(pm, g, s), a)
    a = P.dve(copy(m, pm), a)
    a = P.dve(ts(x, x, m, None, ALU.subtract), a)
    a = P.act(act(scratch, x, ACT.Square, accum_out=v), a)
    a = P.pe(mm(pm, g, v), a)
    a = P.act(act(r, pm, ACT.Sqrt, bias=K["eps5"][0:C, :]), a)
    a = P.dve(lambda e: e.reciprocal(s, r), a)
    return P.dve(ts(x, x, s, None, ALU.mult), a)



def attention(P, K, D, src, dst):
    PS = P.PS
    KT = [(t * 128, min(128, L - t * 128)) for t in range(25)]
    scale = float(C) ** -0.5
    with ExitStack() as ctx:
        sb = lambda n, s, d=F32: P.sb(ctx, n, s, d)
        wqk, wv = sb("wqk", [C, C]), sb("wv", [C, 48])
        wp, bp = sb("wp", [16, 3, C]), sb("bp", [C, 1])
        xres, xg = sb("xres", [C, L]), sb("xg", [C, L])
        parts = [sb(f"part{i}", [C, L], BF16) for i in range(3)]
        rem = sb("rem", [C, 2, T])
        Q = [sb(f"Q{h}", [99, L], BF16) for h in range(3)]
        KK = [sb(f"K{h}", [99, L], BF16) for h in range(3)]
        V = sb("V", [128, 25, 3, 48])
        NP = 3
        Pr = sb("Pr", [128, NP, 3, T])
        mx = sb("mx", [128, 25, 2])
        mm1, mr, mr2 = sb("mm1", [128, 25]), sb("mr", [128, 25]), sb("mr2", [128, 25])
        nm = sb("nm", [128, 25, 3], BF16)
        rec, oh = sb("rec", [16, T]), sb("oh", [16, 3, T])
        yo = sb("yo", [C, 2, T])
        small = sb("small", [128, 8])
        w = [P.dma(wqk[:], D["wqk"]), P.dma(wv[:], D["wv"]), P.dma(wp[:], D["wp"]), P.dma(bp[:], D["bp"])]
        ones = [P.dve(lambda e, h=h: e.memset(KK[h][96:99, :], 1.0)) for h in range(3)]
        vinit = P.pool(lambda e: e.memset(V[:], 0.0))
        vinit = P.pool(lambda e: e.memset(V[:, :, :, 32:48], 1.0), vinit)
        minit = P.dve(lambda e: e.memset(mx[:], 0.0))
        yout = [None, None]
        for b in range(NI):
            ld = [P.dma(xres[:], src[b], yout), P.dma(xg[:], src[b], P.pe.last)]
            gn = groupnorm(P, K, K["gn"][:], xg[:], 7, ld + [w, P.pe.last], parts[0][:], small)
            evac = [None, None]
            for t in range(NT):
                s, cols = t % 2, slice(t * T, t * T + T)
                p = PS[0:C, s, 0:T]
                a = P.pe(mm(p, wqk[:], xg[:, cols]), gn, evac[s])
                hi = P.act(act(parts[0][:, cols], p, ACT.Copy), a)
                r1 = P.dve(tt(rem[:, s, :], p, parts[0][:, cols], ALU.subtract), hi)
                evac[s] = r1
                mid = P.act(act(parts[1][:, cols], rem[:, s, :], ACT.Copy), r1)
                lo = P.dve(tt(parts[2][:, cols], rem[:, s, :], parts[1][:, cols], ALU.subtract), mid)
            stacked = [[], [], []]
            used = P.pe.last
            for h in range(3):
                for j, (a, c) in enumerate([(0, 0), (0, 1), (1, 0), (1, 1), (0, 2), (2, 0)]):
                    rows = slice(16 * j, 16 * j + 16)
                    stacked[h].append(P.dma(Q[h][rows, :], parts[a][16 * h:16 * h + 16, :], used, mid, lo))
                    stacked[h].append(P.dma(KK[h][rows, :], parts[c][48 + 16 * h:64 + 16 * h, :], used, mid, lo))
            vfree = [None, None]
            for t, (k0, kn) in enumerate(KT):
                s = 2 + t % 2
                p = PS[0:kn, s, 0:48]
                a = P.pe(mm(p, xg[:, k0:k0 + kn], wv[:]), gn, vfree[t % 2], vinit)
                vfree[t % 2] = vready = P.act(
                    act(V[0:kn, t, :, 0:16], p.rearrange("p (h d) -> p h d", h=3), ACT.Copy), a, vinit)
            free = [None, None]
            for h in range(3):
                for t, (q0, qn) in enumerate(KT):
                    for half, (b0, nb) in enumerate([(0, 4), (4, 3)]):
                        for i in range(nb):
                            k0 = (b0 + i) * T
                            a = P.pe(mm(PS[0:qn, b0 + i, 0:T], Q[h][0:96, q0:q0 + qn], KK[h][0:96, k0:k0 + T]),
                                     stacked[h], free[half], evac, vready)
                        free[half] = P.dve(lambda e, o=mx[0:qn, t, half:half + 1], i_=PS[0:qn, b0:b0 + nb, 0:T]:
                                           e.tensor_reduce(o, i_, AX.XY, ALU.max), a, minit)
                a = P.dve(tt(mm1[:], mx[:, :, 0], mx[:, :, 1], ALU.max), free)
                a = P.dve(ts(mr[:], mm1[:], -1.0, None, ALU.mult), a)
                a = P.dve(copy(nm[:, :, 0], mr[:]), a, P.pe.last)
                a = P.dve(tt(mr2[:], mr[:], nm[:, :, 0], ALU.subtract), a)
                a = P.dve(copy(nm[:, :, 1], mr2[:]), a)
                a = P.dve(tt(nm[:, :, 2], mr2[:], nm[:, :, 1], ALU.subtract), a)
                for g in range(7):
                    tiles = list(range(4 * g, min(4 * g + 4, 25)))
                    n = 0
                    for t in tiles:
                        kn = KT[t][1]
                        c = P.pe(mm(PS[0:3, 7, n:n + kn], nm[:, t, :], K["identb"][:, 0:kn]), a,
                                 P.act.last if t == tiles[0] else None)
                        n += kn
                    q0 = KT[tiles[0]][0]
                    mrow = P.act(act(Q[h][96:99, q0:q0 + n], PS[0:3, 7, 0:n], ACT.Copy), c)
            groups = [list(range(g, min(g + 3, 25))) for g in range(0, 25, 3)]
            banks, pfree = [free, free], [None] * NP
            n = 0
            ofree = None
            yfree = None
            for qc in range(NT):
                cols = slice(qc * T, qc * T + T)
                ohs = []
                for h in range(3):
                    todo = []

                    def pv(item, last):
                        tiles, slot, ready = item
                        for i, t in enumerate(tiles):
                            kn = KT[t][1]
                            a = P.pe(mm(PS[0:48, 6, 0:T], V[0:kn, t, h, :], Pr[0:kn, slot, i, :],
                                        start=(t == 0), stop=(t == 24)), ready, vready, ofree if t == 0 else None)
                        pfree[slot] = a
                        return a

                    for gi, tiles in enumerate(groups):
                        s, slot = n % 2, n % NP
                        kn = KT[tiles[0]][1]
                        for i, t in enumerate(tiles):
                            k0 = KT[t][0]
                            a = P.pe(mm(PS[0:kn, 3 * s + i, 0:T], KK[h][0:99, k0:k0 + kn], Q[h][0:99, cols]),
                                     mrow, ones, banks[s])
                        banks[s] = P.act(act(Pr[0:kn, slot, 0:len(tiles), :],
                                             PS[0:kn, 3 * s:3 * s + len(tiles), 0:T], ACT.Exp, scale=scale),
                                         a, pfree[slot])
                        todo.append((tiles, slot, banks[s]))
                        n += 1
                        if len(todo) == 2:
                            pv(todo.pop(0), False)
                    o = pv(todo.pop(0), True)
                    a = P.dve(lambda e: e.reciprocal(rec[:], PS[32:48, 6, 0:T]), o)
                    ofree = P.dve(tt(oh[:, h, :], PS[0:16, 6, 0:T], rec[:], ALU.mult), a, yfree)
                    ohs.append(ofree)
                for h in range(3):
                    a = P.pe(mm(PS[0:C, 7, 0:T], wp[:, h, :], oh[:, h, :], start=(h == 0), stop=(h == 2)), ohs,
                             yout[qc % 2] if 0 else None, mrow, P.dve.last)
                yfree = a
                s = qc % 2
                a = P.dve(stt(yo[:, s, :], PS[0:C, 7, 0:T], bp[:], xres[:, cols], ALU.add, ALU.add), a, yout[s], ld)
                yout[s] = P.dma(dst[b][:, cols], yo[:, s, :], a)
            P.barrier()
        P.barrier()



def pieces(order, j, w):
    j8 = 8 * j
    if order == 0:
        return [(j8 * w, [[w, 8], [1, 56]], 0, [[56, 8], [1, 56]])]
    if order == 1:
        return [(j8, [[1, 8], [w, 56]], 0, [[56, 8], [1, 56]])]
    step, n1 = (w + 1, 56 - j8) if order == 2 else (w - 1, j8 + 1)
    wrap = -56 if order == 2 else 56
    out = [(j8, [[1, 8], [step, n1]], 0, [[56, 8], [1, n1]])]
    if n1 < 56:
        out.append((j8 + wrap + n1 * step, [[1, 8], [step, 56 - n1]], n1, [[56, 8], [1, 56 - n1]]))
    return out


def run_dims(off, dims, rev):
    return (T - 1 - off, [[-s, n] for s, n in dims]) if rev else (off, dims)


class Layer:

    def __init__(self, pre, ratio, scans, width, dup):
        self.pre, self.ratio, self.scans, self.width, self.dup = pre, ratio, scans, width, dup


L1 = Layer("l1", False, [(0, False), (1, False), (0, True), (1, True), (2, False), (3, False), (2, True), (3, True)], 64, 8)
L3 = Layer("l3", True, [(0, False), (0, True), (1, False), (1, True)], 56, 0)


def front(P, K, D, lay, pair, src, xc, zd):
    PS, pre = P.PS, lay.pre
    w = lay.width
    with ExitStack() as ctx:
        sb = lambda n, s, d=F32: P.sb(ctx, n, s, d)
        win = sb("win", [C, 384])
        cw, cb = sb("cw", [128, 3, 9]), sb("cb", [128, 3])
        diag = sb("diag", [128, 3, 9, 128])
        xg = [sb(f"xg{i}", [C, L]) for i in range(2)]
        pad = sb("pad", [128, 3, 58, 58])
        zst = sb("zst", [128, 3, T])
        junk = sb("junk", [C, L], BF16)
        small = sb("small", [128, 8])
        lw = [P.dma(win[:], D[pre + "win"]), P.dma(cw[:], D[pre + "cw"]), P.dma(cb[:], D[pre + "cb"])]
        z0 = P.pool(lambda e: e.memset(pad[:], 0.0))
        ld = [P.dma(xg[i][:], src[2 * pair + i]) for i in range(2)]
        dg = None
        for c in range(3):
            for k in range(9):
                dg = P.pool(ts(diag[:, c, k, :], K["ident"][:], cw[:, c, k:k + 1], None, ALU.mult), lw)
        gn = []
        for i in range(2):
            gn.append(groupnorm(P, K, K["gn"][:], xg[i][:], 7, [ld[i], P.pe.last, gn[-1:]], junk[:], small))
        free = [None] * 4
        n = 0
        zout = [None] * 3
        for t in range(NT):
            for c in range(6):
                s = n % 4
                n += 1
                for i in range(2):
                    a = P.pe(mm(PS[64 * i:64 * i + 64, s, 0:T], win[:, 64 * c:64 * c + 64], xg[i][:, t * T:t * T + T]),
                             gn, lw, free[s])
                if c < 3:
                    free[s] = inpad = P.act(act(pad[:, c, 1 + 8 * t:9 + 8 * t, 1:57],
                                                PS[:, s, 0:T].rearrange("p (a b) -> p a b", b=56), ACT.Copy), a, z0)
                else:
                    fn = ACT.Copy if lay.ratio else ACT.Silu
                    free[s] = a = P.act(act(zst[:, c - 3, :], PS[:, s, 0:T], fn), a, zout[c - 3])
                    zout[c - 3] = P.dma(zd[pair, :, c - 3, t * T:t * T + T], zst[:, c - 3, :], a)
        for c in range(3):
            for t in range(NT):
                s = n % 4
                n += 1
                for k in range(9):
                    dy, dx = k // 3, k % 3
                    a = P.pe(mm(PS[:, s, 0:T], diag[:, c, k, :], pad[:, c, 8 * t + dy:8 * t + dy + 8, dx:dx + 56],
                                start=(k == 0), stop=(k == 8)), inpad, dg, free[s])
                o = view(xc, c * H * w + 8 * t * w, [[w, 8], [1, 56]])
                free[s] = a = P.act(act(o, PS[:, s, 0:T].rearrange("p (a b) -> p a b", b=56), ACT.Silu,
                                        bias=cb[:, c:c + 1]), a)
            if lay.dup:
                P.pool(copy(view(xc, c * H * w + 56, [[w, 56], [1, 8]]), view(xc, c * H * w, [[w, 56], [1, 8]])), a)
        P.barrier()


def scans(P, K, D, lay, pair, xc, yacc):
    PS, pre, w = P.PS, lay.pre, lay.width
    NK = len(lay.scans)
    ratio = lay.ratio
    if ratio:
        BA, BW, BC, BY, BX = [0, 1], [2, 3], [4, 5], [6], [7]
    else:
        BA, BC, BY, BX = [0, 1], [2, 3], [4, 5], [6, 7]
    with ExitStack() as ctx:
        sb = lambda n, s, d=F32: P.sb(ctx, n, s, d)
        xp = sb("xp", [128, 2, 3, 204])
        dw = sb("dw", [12, 2, 3, 128])
        A = sb("A", [128, NK, 3, 16])
        db = sb("db", [128, NK, 3])
        ds = sb("ds", [128, 3, NK])
        dsum = sb("dsum", [128, 3])
        xs, dl, du = sb("xs", [128, 2, 3, T]), sb("dl", [128, 2, 3, T]), sb("du", [128, 2, 3, T])
        if ratio:
            cs = sb("cs", [128, 2, 3, T])
            one = K["one"][:, 0:1].broadcast_to([128, T])
            A2 = sb("A2", [128, NK, 3, 16])
            NT2 = 3
            T2 = sb("T2", [128, NT2, T])
        dts = sb("dts", [12, T])
        tmp = [sb(f"tmp{i}", [128, T]) for i in range(4)]
        SB_, SC = sb("SB", [C, T], BF16), sb("SC", [C, 2, T], BF16)
        mt = sb("mt", [C, T], BF16)
        rt = sb("rt", [C, T])
        Bs = sb("Bs", [128, 16, T])
        NTR, NH, NHC = 4, 8, 4
        Tr, Hr, Hc = sb("Tr", [128, NTR, T]), sb("Hr", [128, NH, T]), sb("Hc", [128, NHC, T])
        st = sb("st", [128, 48])

        ld = [P.dma(A[:], D[pre + "A"]), P.dma(db[:], D[pre + "db"]), P.dma(ds[:], D[pre + "ds"])]
        la = ld
        if not ratio:
            a = P.act(act(A[:], A[:], ACT.Exp), ld)
            la = a = P.dve(ts(A[:], A[:], -1.0, None, ALU.mult), a)
        else:
            a = P.dve(ts(A2[:], A[:], 0.5, None, ALU.mult), ld)
            a = P.dve(ts(A[:], A[:], -1.0, None, ALU.mult), a)
            la = P.dve(ts(A2[:], A2[:], -1.0, None, ALU.mult), a)
        a = P.dve(lambda e: e.reduce_sum(dsum[:], ds[:], axis=AX.X), ld)
        n = H * w
        for c in range(3):
            if ratio:
                z = P.dve(lambda e, c=c: e.memset(yacc[:, c * n:(c + 1) * n], 0.0), a)
                ini = P.dve(ts(yacc[:, c * n:(c + 1) * n], yacc[:, c * n:(c + 1) * n], dsum[:, c:c + 1], None, ALU.add), z)
            else:
                ini = P.dve(ts(yacc[:, c * n:(c + 1) * n], xc[:, c * n:(c + 1) * n], dsum[:, c:c + 1], None, ALU.mult), a)
        if lay.dup:
            ini = P.dve(lambda e: e.memset(view(yacc, 56, [[w, 3 * H], [1, w - 56]]), 0.0), ini)

        NC_ = NK * NT
        NU = NC_ * 48
        tA, tC, tT, tS, tH, tY, tW, tT2 = ([None] * NU for _ in range(8))
        dlready, duready, csready = [None] * NC_, [None] * NC_, [None] * NC_
        scready, wld = [None] * NC_, [None] * NK
        bready = {}
        bxfree = [None] * len(BX)
        nbx = [0]
        tmpfree = [None] * 4
        misc = {"dts": None, "rt": None, "SB": None, "mt": None}
        carry = {}
        yev = {}
        yevlast = [ini]

        def bx():
            s = nbx[0] % len(BX)
            nbx[0] += 1
            return s

        def load(k):
            s = k % 2
            wld[k] = [P.dma(xp[:, s], D[pre + "xp"][k], P.pe.last), P.dma(dw[:, s], D[pre + "dw"][k], P.pe.last)]

        def steps(q):
            k, j = divmod(q, NT)
            order, rev = lay.scans[k]
            jj = NT - 1 - j if rev else j
            s, ks = q % 2, k % 2
            X = xs[:, s]
            if j == 0:
                load(k)
            old = [tA[48 * (q - 1) - 1], tT[48 * (q - 1) - 1], tW[48 * (q - 1) - 1]] if q >= 2 else []

            def gather():
                for off, dims, ro, rd in pieces(order, jj, w):
                    ro, rd = run_dims(ro, rd, rev)
                    for c in range(3):
                        g = P.act(act(view(xs, (s * 3 + c) * T + ro, rd), view(xc, c * n + off, dims), ACT.Copy),
                                  duready[q - 2] if q >= 2 else None, scready[q - 2] if q >= 2 else None)
                misc["g"] = g

            def proj(out, cols, waits):
                for c in range(3):
                    a = P.pe(mm(out, xp[:, ks, c, cols], X[:, c, :], start=(c == 0), stop=(c == 2)),
                             misc["g"], wld[k], waits)
                return a

            def dt():
                b = bx()
                p = PS[0:12, BX[b], 0:T]
                a = proj(p, slice(192, 204), bxfree[b])
                bxfree[b] = misc["dts"] = P.act(act(dts[:], p, ACT.Copy), a, misc.get("dtsused"))

            def delta(c):
                def first():
                    b = bx()
                    p = PS[:, BX[b], 0:T]
                    a = P.pe(mm(p, dw[:, ks, c, :], dts[:]), misc["dts"], wld[k], bxfree[b])
                    misc["dtsused"] = a
                    P.act(act(tmp[0][:], p, ACT.Abs, bias=db[:, k, c:c + 1]), a, ld, tmpfree[0])
                    bxfree[b] = P.act(act(tmp[1][:], p, ACT.Relu, bias=db[:, k, c:c + 1]), tmpfree[1])
                    P.act.wait(P.act.last)
                    misc["e"] = P.act(act(tmp[0][:], tmp[0][:], ACT.Exp, scale=-1.0))
                    P.act.wait(P.act.last)
                    misc["l"] = P.act(act(tmp[2][:], tmp[0][:], ACT.Ln, bias=K["one"][:]), tmpfree[2])

                def second():
                    a = P.dve(ts(tmp[3][:], tmp[0][:], 1.0, 1.0, ALU.add, ALU.subtract), misc["e"])
                    b_ = P.dve(tt(tmp[1][:], tmp[1][:], tmp[2][:], ALU.add), misc["l"])
                    a = P.dve(tt(tmp[3][:], tmp[0][:], tmp[3][:], ALU.subtract), a)
                    a = P.dve(tt(dl[:, s, c, :], tmp[1][:], tmp[3][:], ALU.add), a, b_, old)
                    for i in range(4):
                        tmpfree[i] = a
                    dlready[q] = a
                return [first, second]

            def mult():
                if ratio:
                    duready[q] = P.dve(stt(du[:, s], dl[:, s], 0.5, X, ALU.mult, ALU.mult), dlready[q], misc["g"], old)
                else:
                    duready[q] = P.dve(tt(du[:, s], dl[:, s], X, ALU.mult), dlready[q], misc["g"], old)

            def cumsum(c):
                init = 0.0 if j == 0 else cs[:, 1 - s, c, T - 1:T]
                csready[q] = P.dve(lambda e: e.tensor_tensor_scan(cs[:, s, c, :], one, dl[:, s, c, :], init,
                                                                 ALU.mult, ALU.add),
                                   dlready[q], csready[q - 1] if q else None, old, la)

            def split(dst, cols, key):
                def first():
                    b = bx()
                    p = PS[0:C, BX[b], 0:T]
                    a = proj(p, cols, bxfree[b])
                    h = P.act(act(dst[:], p, ACT.Copy), a, misc.get(key))
                    bxfree[b] = misc["r1"] = P.dve(tt(rt[:], p, dst[:], ALU.subtract), h, misc.get("rtused"))

                def second():
                    a = P.act(act(dst[32:64, :], rt[32:64, :], ACT.Copy), misc["r1"])
                    a = P.act(act(mt[64:96, :], rt[64:96, :], ACT.Copy), misc.get("rtused"))
                    misc[key + "r"] = misc["rtused"] = P.dve(
                        tt(dst[64:96, :], rt[64:96, :], mt[64:96, :], ALU.subtract), a)
                return [first, second]

            def cdone():
                scready[q] = misc["SCr"]

            misc["SC"] = tC[48 * (q - 1) - 1] if q >= 2 else None
            out = [gather, dt]
            cdst = SC[:, s, :]
            out += [lambda: misc.__setitem__("SC", tC[48 * (q - 1) - 1] if q >= 2 else None)]
            out += split(cdst, slice(96, 192), "SC")
            for c in range(3):
                out += delta(c)
            out += [mult]
            if ratio:
                out += [lambda c=c: cumsum(c) for c in range(3)]
            out += split(SB_[:], slice(0, 96), "SB") + [cdone]
            return out

        def bstep(q, nn):
            b = bx()
            p = PS[:, BX[b], 0:T]
            a = P.pe(mm(p, K["sel"][:, nn, :], SB_[:]), misc["SBr"], bxfree[b])
            if nn == 15:
                misc["SB"] = a
            bxfree[b] = bready[(q, nn)] = P.act(act(Bs[:, nn, :], p, ACT.Copy), a, tT[48 * (q - 1) + 32 + nn] if q else None)

        def uT(i):
            q, r = divmod(i, 48)
            c, nn = divmod(r, 16)
            tT[i] = P.pool(tt(Tr[:, i % NTR, :], du[:, q % 2, c, :], Bs[:, nn, :], ALU.mult),
                           duready[q], bready[(q, nn)], (tT2 if ratio else tS)[i - NTR] if i >= NTR else None)

        def uA(i):
            q, r = divmod(i, 48)
            c, nn = divmod(r, 16)
            k = q // NT
            tA[i] = P.act(act(PS[:, BA[i % 2], 0:T], dl[:, q % 2, c, :], ACT.Exp, scale=A[:, k, c, nn:nn + 1]),
                          dlready[q], la, tS[i - 2] if i >= 2 else None)

        def uW(i):
            q, r = divmod(i, 48)
            c, nn = divmod(r, 16)
            k = q // NT
            tW[i] = P.act(act(PS[:, BW[i % 2], 0:T], cs[:, q % 2, c, :], ACT.Tanh, scale=A2[:, k, c, nn:nn + 1],
                              bias=K["lneps"][:]), csready[q], la, tT2[i - 2] if i >= 2 else None)

        def uT2(i):
            tT2[i] = P.dve(stt(T2[:, i % NT2, :], PS[:, BW[i % 2], 0:T], 1.0, Tr[:, i % NTR, :], ALU.add, ALU.mult),
                           tW[i], tT[i], tS[i - NT2] if i >= NT2 else None)

        def uC(i):
            q, r = divmod(i, 48)
            nn = r % 16
            tC[i] = P.pe(mm(PS[:, BC[i % 2], 0:T], K["sel"][:, nn, :], SC[:, q % 2, :]),
                         scready[q], tH[i - 2] if i >= 2 else None)

        def uS(i):
            q, r = divmod(i, 48)
            j = q % NT
            init = 0.0 if j == 0 else st[:, r:r + 1]
            inp = T2[:, i % NT2, :] if ratio else Tr[:, i % NTR, :]
            tS[i] = P.dve(lambda e: e.tensor_tensor_scan(Hr[:, i % NH, :], PS[:, BA[i % 2], 0:T], inp, init,
                                                         ALU.mult, ALU.add),
                          tA[i], tT2[i] if ratio else tT[i], tH[i - NH] if i >= NH else None,
                          carry.get((q - 1, r // 4)) if j else None, carry.get(divmod(i - NH, 48)[0:1] + (((i - NH) % 48) // 4,)))
            if i % 4 == 3:
                carry[(q, r // 4)] = P.act(act(st[:, r - 3:r + 1], view(Hr, (i - 3) % NH * T + T - 1, [[T, 4]]), ACT.Copy), tS[i])

        def uH(i):
            tH[i] = P.dve(tt(Hc[:, i % NHC, :], PS[:, BC[i % 2], 0:T], Hr[:, i % NH, :], ALU.mult),
                          tS[i], tC[i], tY[i - NHC] if i >= NHC else None)

        def uY(i):
            q, r = divmod(i, 48)
            c, nn = divmod(r, 16)
            g = 3 * q + c
            tY[i] = P.pe(mm(PS[:, BY[g % len(BY)], 0:T], K["ident"][:], Hc[:, i % NHC, :], start=(nn == 0), stop=(nn == 15)),
                         tH[i], yev.get(g - len(BY)) if nn == 0 else None)

        def uE(g):
            q, c = divmod(g, 3)
            k, j = divmod(q, NT)
            order, rev = lay.scans[k]
            jj = NT - 1 - j if rev else j
            for off, dims, ro, rd in pieces(order, jj, w):
                ro, rd = run_dims(ro, rd, rev)
                o = view(yacc, c * n + off, dims)
                i_ = view(PS[:, BY[g % len(BY)], :], ro, rd)
                a = P.dve(tt(o, i_, o, ALU.add), tY[16 * g + 15], yevlast[0])
            yevlast[0] = yev[g] = a

        for f in steps(0):
            f()
        for nn in range(16):
            bstep(0, nn)
        for i in range(2):
            uT(i)
        if ratio:
            uW(0)
            uW(1)
            uT2(0)
        uA(0)
        uC(0)
        pend = []
        todo = []
        for i in range(NU):
            q, r = divmod(i, 48)
            if r == 0:
                assert not todo
                todo = steps(q + 1) if q + 1 < NC_ else []
                total, done = len(todo), 0
            if i + 2 < NU:
                uT(i + 2)
            if i + 1 < NU:
                uA(i + 1)
            if ratio:
                if i + 2 < NU and i >= 1:
                    pass
                if i + 1 < NU:
                    uT2(i + 1)
                if i + 3 < NU + 1 and i + 2 < NU:
                    uW(i + 2)
            uS(i)
            if i >= 1:
                uH(i - 1)
                uY(i - 1)
                if (i - 1) % 16 == 15:
                    pend.append((i if ratio else i + 2, (i - 1) // 16))
            if i + 1 < NU:
                uC(i + 1)
            if pend and pend[0][0] <= i:
                uE(pend.pop(0)[1])
            while todo and done < total * (r + 1) / 30:
                todo.pop(0)()
                done += 1
            if r >= 32 and q + 1 < NC_:
                bstep(q + 1, r - 32)
        uH(NU - 1)
        uY(NU - 1)
        for _, g in pend:
            uE(g)
        uE(NU // 16 - 1)
        P.barrier()
        if lay.dup:
            a = P.dve(tt(view(yacc, 0, [[w, 3 * H], [1, 8]]), view(yacc, 0, [[w, 3 * H], [1, 8]]),
                         view(yacc, 56, [[w, 3 * H], [1, 8]]), ALU.add))
            P.barrier()


def tail_norm(P, K, sb, yacc, w):
    PS = P.PS
    rstd = sb("rstd", [128, L])
    sq = sb("sq", [128, 2, 3, T])
    sd = sb("sd", [128, 2, T])
    free, vfree, sqfree = [None, None], [None, None], [None, None]
    n = H * w
    for t in range(NT):
        s = t % 2
        y3 = view(yacc, 8 * t * w, [[n, 3], [w, 8], [1, 56]])
        for c in range(3):
            a = P.pe(mm(PS[:, s, 0:T], K["blk"][:], view(yacc, c * n + 8 * t * w, [[w, 8], [1, 56]]),
                        start=(c == 0), stop=(c == 2)), free[s])
        for c in range(3):
            yc = view(yacc, c * n + 8 * t * w, [[w, 8], [1, 56]])
            a = P.dve(tt(yc, yc, PS[:, s, 0:T].rearrange("p (a b) -> p a b", b=56), ALU.subtract), a)
        free[s] = a
        for c in range(3):
            a2 = P.act(act(sq[:, s, c, :].rearrange("p (a b) -> p a b", b=56),
                           view(yacc, c * n + 8 * t * w, [[w, 8], [1, 56]]), ACT.Square), a, sqfree[s])
        for c in range(3):
            a = P.pe(mm(PS[:, 2 + s, 0:T], K["blk"][:], sq[:, s, c, :], start=(c == 0), stop=(c == 2)), a2, vfree[s])
        sqfree[s] = a
        a = P.act(act(sd[:, s, :], PS[:, 2 + s, 0:T], ACT.Sqrt, bias=K["eps5"][:]), a, vfree[s])
        vfree[s] = r = P.dve(lambda e, t=t, s=s: e.reciprocal(rstd[:, t * T:t * T + T], sd[:, s, :]), a)
    return rstd, r


def gated(P, K, sb, ctx_ld, zd, pair, yacc, w, rstd, ready, lg, lb):
    z = sb("z", [128, 2, 3, T])
    zfree = [None, None]
    n = H * w
    out = []
    for t in range(NT):
        s = t % 2
        lz = P.dma(z[:, s], zd[pair, :, :, t * T:t * T + T], zfree[s])
        for c in range(3):
            yc = view(yacc, c * n + 8 * t * w, [[w, 8], [1, 56]])
            r = rstd[:, t * T:t * T + T].rearrange("p (a b) -> p a b", b=56)
            a = P.dve(tt(yc, yc, r, ALU.mult), ready)
            a = P.dve(ts(yc, yc, lg[:, c:c + 1], lb[:, c:c + 1], ALU.mult, ALU.add), a, ctx_ld)
            a = P.dve(tt(yc, yc, z[:, s, c, :].rearrange("p (a b) -> p a b", b=56), ALU.mult), a, lz)
        zfree[s] = a
        out.append(a)
    return out


def tail1(P, K, D, pair, src, dst, yacc, zd):
    PS, w = P.PS, L1.width
    with ExitStack() as ctx:
        sb = lambda n, s, d=F32: P.sb(ctx, n, s, d)
        wo, lg, lb = sb("wo", [128, 3, C]), sb("lg", [128, 3]), sb("lb", [128, 3])
        ld = [P.dma(wo[:], D["l1wo"]), P.dma(lg[:], D["l1lg"]), P.dma(lb[:], D["l1lb"])]
        rstd, r = tail_norm(P, K, sb, yacc, w)
        g = gated(P, K, sb, ld, zd, pair, yacc, w, rstd, r, lg, lb)
        xr, yo = sb("xr", [C, 4, T]), sb("yo", [C, 4, T])
        free, bfree = [None] * 4, [None] * 2
        n = H * w
        for t in range(NT):
            for i in range(2):
                u = 2 * t + i
                s = u % 4
                img, cols = 2 * pair + i, slice(t * T, t * T + T)
                lx = P.dma(xr[:, s, :], src[img][:, cols], free[s])
                p = PS[0:C, 4 + u % 2, 0:T]
                for c in range(3):
                    rhs = view(yacc, c * n + 8 * t * w, [[w, 8], [1, 56]])[64 * i:64 * i + 64]
                    a = P.pe(mm(p, wo[64 * i:64 * i + 64, c, :], rhs, start=(c == 0), stop=(c == 2)),
                             g[t], ld, bfree[u % 2])
                bfree[u % 2] = a = P.dve(tt(yo[:, s, :], p, xr[:, s, :], ALU.add), a, lx, free[s])
                free[s] = P.dma(dst[img][:, cols], yo[:, s, :], a)
        P.barrier()


def bnfold(P, K, sb, name, D, key, bias, n, waits):
    t = sb(name, [128, 4, n])
    o = sb(name + "o", [128, 2, n])
    ld = [P.dma(t[:], D[key]), waits]
    a = P.act(act(o[:, 0], t[:, 3], ACT.Sqrt, bias=K["eps5"][:]), ld)
    a = P.dve(lambda e: e.reciprocal(o[:, 1], o[:, 0]), a)
    a = P.dve(tt(o[:, 0], o[:, 1], t[:, 0], ALU.mult), a)
    b = P.dve(tt(o[:, 1], bias, t[:, 2], ALU.subtract), a)
    b = P.dve(tt(o[:, 1], o[:, 1], o[:, 0], ALU.mult), b)
    b = P.dve(tt(o[:, 1], o[:, 1], t[:, 1], ALU.add), b)
    return o, b


def tail3(P, K, D, pair, src, dst, yacc, zd):
    PS, w = P.PS, L3.width
    n = H * w
    with ExitStack() as ctx:
        sb = lambda n, s, d=F32: P.sb(ctx, n, s, d)
        lg, lb = sb("lg", [128, 3]), sb("lb", [128, 3])
        b1, b2 = sb("b1", [128, 3]), sb("b2", [128, 3])
        ld = [P.dma(lg[:], D["l3lg"]), P.dma(lb[:], D["l3lb"]), P.dma(b1[:], D["c1b"]), P.dma(b2[:], D["c2b"])]
        bn1, t1 = bnfold(P, K, sb, "bn1", D, "bn1", b1[:], 3, ld)
        bn2, t2 = bnfold(P, K, sb, "bn2", D, "bn2", b2[:], 3, ld)
        with ExitStack() as c2:
            sb2 = lambda n, s, d=F32: P.sb(c2, n, s, d)
            rstd, r = tail_norm(P, K, sb2, yacc, w)
            gated(P, K, sb2, ld, zd, pair, yacc, w, rstd, r, lg, lb)
            P.barrier()
        w1, cw, w3 = sb("w1", [128, 3, 384]), sb("cw", [128, 3, 9]), sb("w3", [128, 3, C])
        diag = sb("diag", [128, 3, 9, 128])
        c3b, s1w, s1b = sb("c3b", [C, 1]), sb("s1w", [C, 48]), sb("s1b", [48, 1])
        s2w, s2b = sb("s2w", [48, C]), sb("s2b", [C, 1])
        pad = sb("pad", [128, 3, 58, 58])
        cv = sb("cv", [128, 2, 3, T])
        t3 = sb("t3", [C, L])
        xr = sb("xr", [C, L])
        sums, sm, s1, s2 = sb("sums", [C, NT]), sb("sm", [C, 1]), sb("s1", [48, 1]), sb("s2", [C, 1])
        lw = [P.dma(w1[:], D["c1w"]), P.dma(cw[:], D["c2w"]), P.dma(w3[:], D["c3w"]), P.dma(c3b[:], D["c3b"]),
              P.dma(s1w[:], D["s1w"]), P.dma(s1b[:], D["s1b"]), P.dma(s2w[:], D["s2w"]), P.dma(s2b[:], D["s2b"])]
        z0 = P.pool(lambda e: e.memset(pad[:], 0.0))
        for c in range(3):
            for k in range(9):
                dg = P.pool(ts(diag[:, c, k, :], K["ident"][:], cw[:, c, k:k + 1], None, ALU.mult), lw)
        out = None
        for i in range(2):
            img = 2 * pair + i
            lx = P.dma(xr[:], src[img], out)
            free = [None] * 4
            u = 0
            for c in range(3):
                for t in range(NT):
                    s = u % 4
                    u += 1
                    for cc in range(3):
                        rhs = view(yacc, cc * n + 8 * t * w, [[w, 8], [1, 56]])[64 * i:64 * i + 64]
                        a = P.pe(mm(PS[:, s, 0:T], w1[64 * i:64 * i + 64, cc, 128 * c:128 * c + 128], rhs,
                                    start=(cc == 0), stop=(cc == 2)), lw, free[s])
                    free[s] = inpad = P.act(act(pad[:, c, 1 + 8 * t:9 + 8 * t, 1:57],
                                                PS[:, s, 0:T].rearrange("p (a b) -> p a b", b=56), ACT.Relu,
                                                scale=bn1[:, 0, c:c + 1], bias=bn1[:, 1, c:c + 1]), a, z0, t1, P.pe.last)
            cvfree, ofree = [None] * 2, [None] * 2
            for t in range(NT):
                v = t % 2
                for c in range(3):
                    s = u % 4
                    u += 1
                    for k in range(9):
                        dy, dx = k // 3, k % 3
                        a = P.pe(mm(PS[:, s, 0:T], diag[:, c, k, :], pad[:, c, 8 * t + dy:8 * t + dy + 8, dx:dx + 56],
                                    start=(k == 0), stop=(k == 8)), inpad, dg, free[s])
                    free[s] = b = P.act(act(cv[:, v, c, :], PS[:, s, 0:T], ACT.Relu,
                                            scale=bn2[:, 0, c:c + 1], bias=bn2[:, 1, c:c + 1]), a, t2, cvfree[v])
                p = PS[0:C, 4 + v, 0:T]
                for c in range(3):
                    a = P.pe(mm(p, w3[:, c, :], cv[:, v, c, :], start=(c == 0), stop=(c == 2)), b, ofree[v])
                cvfree[v] = a
                ofree[v] = a = P.act(act(t3[:, t * T:t * T + T], p, ACT.Identity, bias=c3b[:],
                                         accum_out=sums[:, t:t + 1]), a, out, P.dve.last)
            a = P.dve(lambda e: e.reduce_sum(sm[:], sums[:], axis=AX.X), a, P.act.last)
            b = P.pe(mm(PS[0:48, 6, 0:1], s1w[:], sm[:]), a)
            a = P.act(act(s1[:], PS[0:48, 6, 0:1], ACT.Relu, bias=s1b[:], scale=1.0 / L), b)
            b = P.pe(mm(PS[0:C, 7, 0:1], s2w[:], s1[:]), a)
            a = P.act(act(s2[:], PS[0:C, 7, 0:1], ACT.Sigmoid, bias=s2b[:]), b)
            a = P.dve(ts(s2[:], s2[:], 1.0, None, ALU.add), a)
            a = P.dve(stt(xr[:], t3[:], s2[:], xr[:], ALU.mult, ALU.add), a, lx)
            out = P.dma(dst[img], xr[:], a)
        P.barrier()


def ssm(P, K, D, lay, src, dst, zd):
    w = lay.width
    for pair in range(2):
        with ExitStack() as ctx:
            yacc = P.sb(ctx, "yacc", [128, 3 * H * w])
            with ExitStack() as c2:
                xc = P.sb(c2, "xc", [128, 3 * H * w])
                front(P, K, D, lay, pair, src, xc, zd)
                scans(P, K, D, lay, pair, xc, yacc)
            (tail3 if lay.ratio else tail1)(P, K, D, pair, src, dst, yacc, zd)



def local(P, K, D, src, dst):
    PS = P.PS
    with ExitStack() as ctx:
        sb = lambda n, s, d=F32: P.sb(ctx, n, s, d)
        w1, b1, w2, b2 = sb("w1", [C, 192]), sb("b1", [C, 2]), sb("w2", [C, 2, C]), sb("b2", [C, 1])
        lg, lb = sb("lg", [C, 1]), sb("lb", [C, 1])
        mask = sb("mask", [112, 30 * 56])
        xres, xg, xn, xl = (sb(f"x{i}", [C, L]) for i in "rgnl")
        FE = sb("FE", [112, 55, C])
        t0, t1_, t2_, t3_ = (sb(f"t{i}", [C, 2, T]) for i in range(4))
        S, R, E = sb("S", [112, 2, 2, T]), sb("R", [112, 2, 2, T]), sb("E", [112, 2, 2, T])
        WT = sb("WT", [112, 2, 8, 112])
        m8, nb, den = sb("m8", [112, 2, 8]), sb("nb", [112, 2]), sb("den", [112, 2, 2])
        hid = sb("hid", [C, 2, 2, T])
        yo = sb("yo", [C, 2, T])
        small = sb("small", [128, 8])
        ld = [P.dma(a[:], D[k]) for a, k in ((w1, "w1"), (b1, "b1"), (w2, "w2"), (b2, "b2"), (lg, "l2lg"),
                                             (lb, "l2lb"), (mask, "mask"))]
        for b in range(NI):
            lx = [P.dma(xres[:], src[b]), P.dma(xg[:], src[b])]
            gn = groupnorm(P, K, K["gn"][:], xg[:], 7, [lx, P.pe.last], xn[:], small)
            for t in range(NT):
                s, cols = t % 2, slice(t * T, t * T + T)
                P.act.wait(P.dve.last, P.pe.last)
                P.dve.wait(P.pe.last)
                a = P.act(act(t0[:, s, :], xg[:, cols], ACT.Square), gn)
                a = P.pe(mm(PS[0:C, s, 0:T], K["ones"][0:C, 0:C], t0[:, s, :]), a)
                a = P.act(act(t1_[:, s, :], PS[0:C, s, 0:T], ACT.Sqrt), a)
                a = P.dve(ts(t1_[:, s, :], t1_[:, s, :], 1e-12, None, ALU.max), a)
                a = P.dve(lambda e, s=s: e.reciprocal(t1_[:, s, :], t1_[:, s, :]), a)
                P.dve(tt(xn[:, cols], xg[:, cols], t1_[:, s, :], ALU.mult), a)
                a = P.pe(mm(PS[0:C, 2 + s, 0:T], K["mean96"][0:C, 0:C], xg[:, cols]), gn)
                a = P.dve(tt(xl[:, cols], xg[:, cols], PS[0:C, 2 + s, 0:T], ALU.subtract), a)
                a = P.act(act(t2_[:, s, :], xl[:, cols], ACT.Square), a)
                a = P.pe(mm(PS[0:C, 4 + s, 0:T], K["mean96"][0:C, 0:C], t2_[:, s, :]), a)
                a = P.act(act(t3_[:, s, :], PS[0:C, 4 + s, 0:T], ACT.Sqrt, bias=K["eps5"][0:C, :]), a)
                a = P.dve(lambda e, s=s: e.reciprocal(t3_[:, s, :], t3_[:, s, :]), a)
                a = P.dve(tt(xl[:, cols], xl[:, cols], t3_[:, s, :], ALU.mult), a)
                a = P.dve(ts(xl[:, cols], xl[:, cols], lg[:], lb[:], ALU.mult, ALU.add), a, ld)
            P.barrier()
            free = [None, None]
            for i in range(55):
                r0 = 2 * i if i < 28 else 2 * (i - 28) + 1
                s = i % 2
                a = P.pe(lambda e, s=s, r0=r0: e.transpose(PS[0:112, s, 0:C], xg[:, 56 * r0:56 * r0 + 112],
                                                            K["ident"][0:C, 0:C]), free[s])
                free[s] = P.act(act(FE[:, i, :], PS[0:112, s, 0:C], ACT.Copy), a)
            P.barrier()
            NQ = 28
            tk = {}

            def front_(t):
                s = t % 2
                y0 = 2 * t
                ks = min(max(y0 - 7, 0), 40)
                mo = (ks - y0 + 14) * 56
                for i in range(2):
                    a = P.pe(mm(PS[0:112, 2 * s + i, 0:T], xn[:, 112 * t:112 * t + 112],
                                xn[:, ks * 56 + T * i:ks * 56 + T * i + T]), tk.get(("S", t - 2)))
                a = P.dve(tt(S[:, s], PS[0:112, 2 * s:2 * s + 2, 0:T],
                             mask[:, mo:mo + 2 * T].rearrange("p (a b) -> p a b", b=T), ALU.add), a, ld,
                          tk.get(("E", t - 2)))
                tk["S", t] = a
                Sf = S[:, s].rearrange("p a b -> p (a b)")
                Rf = R[:, s].rearrange("p a b -> p (a b)")
                Ef = E[:, s].rearrange("p a b -> p (a b)")
                a = P.dve(lambda e: e.max(m8[:, s, :], Sf), a)
                a = P.dve(ts(nb[:, s:s + 1], m8[:, s, 0:1], -1.0, None, ALU.mult), a)
                tk["nb", t] = a
                tk["R", t] = P.dve(lambda e: e.match_replace(Rf, m8[:, s, :], Sf, -3e9), a)
                tk["E", t] = P.act(act(Ef, Sf, ACT.Exp, bias=nb[:, s:s + 1]), tk["nb", t], tk.get(("T", t - 2)))

            def back(t):
                s = t % 2
                ks = min(max(2 * t - 7, 0), 40)
                Rf = R[:, s].rearrange("p a b -> p (a b)")
                Ef = E[:, s].rearrange("p a b -> p (a b)")
                a = P.dve(stt(Ef, Rf, -2e9, Ef, ALU.is_le, ALU.mult, accum_out=den[:, s, 0:1]), tk["E", t], tk["R", t])
                a = P.dve(lambda e: e.reciprocal(den[:, s, 1:2], den[:, s, 0:1]), a)
                a = P.dve(ts(Ef, Ef, den[:, s, 1:2], None, ALU.mult), a)
                for i in range(8):
                    o = PS[0:112, 4 + i // 4, 112 * (i % 4):112 * (i % 4) + 112]
                    a = P.pe(lambda e, o=o, i=i: e.transpose(o, Ef[:, 112 * i:112 * i + 112], K["ident"][0:112, 0:112]),
                             a, tk.get("WT"))
                tk["T", t] = a
                tk["WT"] = a = P.act(act(WT[:, s].rearrange("p (a b) c -> p a (b c)", a=2), PS[0:112, 4:6, 0:T], ACT.Copy),
                                     a, tk.get(("G", t - 2)))
                blk = ks // 2 if ks % 2 == 0 else 28 + (ks - 1) // 2
                for i in range(8):
                    a = P.pe(mm(PS[0:C, 6 + s, 0:112], FE[:, blk + i, :], WT[:, s, i, :], start=(i == 0), stop=(i == 7)),
                             a, tk.get(("X", t - 2)))
                tk["G", t] = a
                tk["X", t] = P.dve(tt(xl[:, 112 * t:112 * t + 112], xl[:, 112 * t:112 * t + 112], PS[0:C, 6 + s, 0:112], ALU.add), a)

            front_(0)
            for t in range(NQ):
                if t + 1 < NQ:
                    front_(t + 1)
                back(t)
            P.barrier()
            hfree, ofree, yf = [None] * 2, [None] * 2, [None] * 2
            for t in range(NT):
                s, cols = t % 2, slice(t * T, t * T + T)
                for i in range(2):
                    p = PS[0:C, 2 * s + i, 0:T]
                    a = P.pe(mm(p, w1[:, C * i:C * i + C], xl[:, cols]), ofree[s])
                    h = P.act(act(hid[:, s, i, :], p, ACT.Relu, bias=b1[:, i:i + 1]), a, hfree[s])
                p = PS[0:C, 4 + s, 0:T]
                for i in range(2):
                    a = P.pe(mm(p, w2[:, i, :], hid[:, s, i, :], start=(i == 0), stop=(i == 1)), h, ofree[s])
                hfree[s] = a
                a = P.dve(stt(yo[:, s, :], p, b2[:], xl[:, cols], ALU.add, ALU.add), a, yf[s])
                ofree[s] = a = P.dve(tt(yo[:, s, :], yo[:, s, :], xres[:, cols], ALU.add), a)
                yf[s] = P.dma(dst[b][:, cols], yo[:, s, :], a)
            P.barrier()
        P.barrier()


def program(nc, D, x, out, stages=(0, 1, 2, 3)):
    with ExitStack() as ctx:
        P = Program(nc, ctx)
        K = {}
        lds = []
        for name, shape in (("ident", [128, 128]), ("gn", [C, C]), ("blk", [128, 128]), ("mean96", [C, C])):
            K[name] = P.sb(ctx, name, shape)
            lds.append(P.dma(K[name][:], D[name]))
        K["sel"] = P.sb(ctx, "sel", [C, 16, 128], BF16)
        K["identb"] = P.sb(ctx, "identb", [128, 128], BF16)
        K["ones"] = P.sb(ctx, "ones", [128, 128])
        P.dve(lambda e: e.memset(K["ones"][:], 1.0))
        for name, v in (("eps5", 1e-5), ("one", 1.0), ("lneps", 13.815510557964274)):
            K[name] = P.sb(ctx, name, [128, 1])
            P.dve(lambda e, t=K[name], v=v: e.memset(t[:], v))
        P.dve(copy(K["identb"][:], K["ident"][:]), lds)
        with ExitStack() as c2:
            self_ = P.sb(c2, "self", [C, 16, 128])
            a = P.dma(self_[:], D["sel"])
            P.dve(copy(K["sel"][:], self_[:]), a)
            P.barrier()
        xd = x.rearrange("b c h w -> b c (h w)")
        od = out.rearrange("b c h w -> b c (h w)")
        zd = nc.dram_tensor("zscratch", (2, 128, 3, L), F32, kind="Internal").ap()
        mid = [nc.dram_tensor(f"mid{i}", (NI, C, L), F32, kind="Internal").ap() for i in range(3)]
        chain = [xd] + mid[:len(stages) - 1] + [od]
        for i, s in enumerate(stages):
            a, b = chain[i], chain[i + 1]
            if s == 0:
                attention(P, K, D, a, b)
            elif s == 1:
                ssm(P, K, D, L1, a, b, zd)
            elif s == 2:
                local(P, K, D, a, b)
            else:
                ssm(P, K, D, L3, a, b, zd)
        P.emit()



def constants():
    g = {}
    g["ident"] = np.eye(128, dtype=np.float32)
    i = np.arange(C)
    g["gn"] = np.where(i[:, None] // 3 == i[None, :] // 3, 1.0 / (3 * L), 0.0).astype(np.float32)
    p = np.arange(128)
    g["blk"] = np.where(p[:, None] // 64 == p[None, :] // 64, 1.0 / 192, 0.0).astype(np.float32)
    g["mean96"] = np.full((C, C), 1.0 / 96, np.float32)
    sel = np.zeros((3, 2, 16, 16, 2, 64), np.float32)
    for n in range(16):
        for m in range(2):
            sel[:, m, n, n, m, :] = 1.0
    g["sel"] = sel.reshape(C, 16, 128)
    q = np.arange(112)
    qy, qx = q // 56, q % 56
    ry = np.arange(-14, 16)
    kx = np.arange(56)
    ok = (abs(ry[None, :, None] - qy[:, None, None]) <= 7) & (abs(kx[None, None, :] - qx[:, None, None]) <= 7)
    g["mask"] = np.where(ok, 0.0, -1e9).astype(np.float32).reshape(112, 30 * 56)
    return g


def paired(a):
    a = np.asarray(a).reshape((3, 64) + np.asarray(a).shape[1:])
    a = np.moveaxis(a, 0, 1)
    return np.ascontiguousarray(np.concatenate([a, a], axis=0))


def scan_weights(pre, g, xp, dw, db, A, ds):
    nk = xp.shape[0]
    o = np.zeros((nk, 2, 64, 3, 204), np.float32)
    for m in range(2):
        for c in range(3):
            blk = np.swapaxes(xp[:, :, 64 * c:64 * c + 64], 1, 2)
            for part in range(3):
                at = 32 * part + 16 * m
                o[:, m, :, c, at:at + 16] = blk[:, :, 6:22]
                o[:, m, :, c, 96 + at:96 + at + 16] = blk[:, :, 22:38]
            o[:, m, :, c, 192 + 6 * m:198 + 6 * m] = blk[:, :, 0:6]
    g[pre + "xp"] = o.reshape(nk, 128, 3, 204)
    d = np.zeros((nk, 2, 6, 3, 2, 64), np.float32)
    for m in range(2):
        d[:, m, :, :, m, :] = np.swapaxes(dw, 1, 2).reshape(nk, 6, 3, 64)
    g[pre + "dw"] = d.reshape(nk, 12, 3, 128)
    g[pre + "A"] = np.ascontiguousarray(np.swapaxes(paired(np.moveaxis(A.reshape(nk, 192, 16), 0, 1)), 1, 2))
    g[pre + "db"] = np.ascontiguousarray(np.swapaxes(paired(np.moveaxis(db.reshape(nk, 192), 0, 1)), 1, 2))
    g[pre + "ds"] = paired(np.moveaxis(ds.reshape(nk, 192), 0, 1))


def layout(v):
    g = constants()
    t = lambda a: np.ascontiguousarray(np.asarray(a).T)
    wq = np.asarray(v["L0_conv_w_qkv"])
    g["wqk"], g["wv"] = t(wq[0:96]), t(wq[96:144])
    g["wp"] = np.ascontiguousarray(np.moveaxis(t(v["L0_conv_w_proj"]).reshape(3, 16, C), 0, 1))
    g["bp"] = np.asarray(v["L0_conv_b_proj"]).reshape(C, 1)
    for pre, s, win in (("l1", "L1_conv_", "w_in"), ("l3", "L3_conv_", "in_proj_w")):
        g[pre + "win"] = t(v[s + win])
        g[pre + "cw"] = paired(np.asarray(v[s + "conv_w"]).reshape(192, 9))
        g[pre + "cb"] = paired(v[s + "conv_b"])
    f = lambda k: np.asarray(v[k])
    scan_weights("l1", g, f("L1_conv_x_proj_weight"), f("L1_conv_dt_projs_weight"), f("L1_conv_dt_projs_bias"),
                 f("L1_conv_A_logs"), f("L1_conv_Ds"))
    scan_weights("l3", g, f("L3_conv_x_proj_w"), f("L3_conv_dt_proj_w"), f("L3_conv_dt_proj_b"),
                 f("L3_conv_A_log"), f("L3_conv_Ds"))
    g["l1lg"], g["l1lb"], g["l1wo"] = paired(f("L1_conv_ln_w")), paired(f("L1_conv_ln_b")), paired(t(f("L1_conv_w_out")))
    g["w1"], g["b1"] = t(f("L2_conv_w1")), t(f("L2_conv_b1").reshape(2, C))
    g["w2"] = np.ascontiguousarray(np.moveaxis(t(f("L2_conv_w2")).reshape(2, C, C), 0, 1))
    g["b2"], g["l2lg"], g["l2lb"] = (f(k).reshape(C, 1) for k in ("L2_conv_b2", "L2_conv_ln_w", "L2_conv_ln_b"))
    g["l3lg"], g["l3lb"] = paired(f("L3_conv_ln_g")), paired(f("L3_conv_ln_b"))
    g["c1w"] = paired(t(f("L3_conv_c1_w").reshape(384, 192)))
    col = lambda a: np.ascontiguousarray(np.moveaxis(a.reshape((3, 128) + a.shape[1:]), 0, 1))
    g["c1b"], g["c2b"] = col(f("L3_conv_c1_b")), col(f("L3_conv_c2_b"))
    g["c2w"] = col(f("L3_conv_c2_w").reshape(384, 9))
    for i in "12":
        g["bn" + i] = np.ascontiguousarray(np.stack([col(f(f"L3_conv_bn{i}_{j}")) for j in "gbmv"], axis=1))
    g["c3w"] = col(t(f("L3_conv_c3_w").reshape(C, 384)))
    g["c3b"] = f("L3_conv_c3_b").reshape(C, 1)
    g["s1w"], g["s1b"] = t(f("L3_conv_se1_w")), f("L3_conv_se1_b").reshape(48, 1)
    g["s2w"], g["s2b"] = t(f("L3_conv_se2_w")), f("L3_conv_se2_b").reshape(C, 1)
    return g


def make(nc, v, stages=(0, 1, 2, 3)):
    arrays = {"x": np.ascontiguousarray(np.asarray(v["x"]))}
    arrays.update(layout(v))
    D = {n: nc.dram_tensor(f"in_{n}", a.shape, F32, kind="ExternalInput").ap() for n, a in arrays.items()}
    out = nc.dram_tensor("out_0", (NI, C, H, W), F32, kind="ExternalOutput").ap()
    program(nc, D, D.pop("x"), out, stages)
    return {f"in_{n}": a for n, a in arrays.items()}


def kernel(**inputs):
    import concourse.bacc as _bacc
    from concourse.bass_utils import run_bass_kernel_spmd as _run

    nc = _bacc.Bacc("TRN2", target_bir_lowering=False, num_devices=1)
    arrays = make(nc, inputs)
    r = _run(nc, [arrays], core_ids=[0])
    return r.results[0]["out_0"]
```

```python
from contextlib import ExitStack

import numpy as np

import concourse.bass as bass
from concourse import mybir

F32 = mybir.dt.float32
BF16 = mybir.dt.bfloat16
ALU = mybir.AluOpType
ACT = mybir.ActivationFunctionType
AX = mybir.AxisListType

H = W = 56
L = H * W
T = 448
NT = L // T
C = 96
NI = 4


class Token:

    def __init__(self, queue, place):
        self.queue, self.place, self.used = queue, place, False


class Landed:

    def __init__(self, slot, value):
        self.slot, self.value = slot, value


class Queue:

    def __init__(self, sem):
        self.sem, self.items, self.last, self.seen = sem, [], None, {}

    def wait(self, *tokens):
        for t in tokens:
            if t is None:
                continue
            if isinstance(t, (list, tuple)):
                self.wait(*t)
            elif isinstance(t, Landed):
                if self.seen.get(t.slot, 0) < t.value:
                    self.seen[t.slot] = t.value
                    self.items.append(("landed", t))
            elif self.seen.get(t.queue, -1) < t.place:
                self.seen[t.queue] = t.place
                t.used = True
                self.items.append(("wait", t))

    def __call__(self, fn, *tokens):
        self.wait(*tokens)
        self.last = Token(self, len(self.items))
        self.items.append(("do", fn, self.last))
        return self.last

    def number(self):
        n = 0
        for item in self.items:
            if item[0] == "do" and item[2].used:
                n += 1
                item[2].value = n

    def emit(self, eng):
        for item in self.items:
            if item[0] == "wait":
                eng.wait_ge(item[1].queue.sem, item[1].value)
            elif item[0] == "landed":
                eng.wait_ge(item[1].slot, item[1].value)
            else:
                done = item[1](eng)
                if item[2].used:
                    done.then_inc(self.sem, 1)


class Program:

    NSLOT = 40

    def __init__(self, nc, ctx):
        self.nc = nc
        self.names = 0
        self.pe, self.act, self.dve, self.pool, self.sp = (
            Queue(ctx.enter_context(nc.semaphore(f"s_{n}"))) for n in ("pe", "act", "dve", "pool", "sp"))
        self.slots = [ctx.enter_context(nc.semaphore(f"s_dma{i}")) for i in range(self.NSLOT)]
        self.landed = [None] * self.NSLOT
        self.ndma = 0
        self.PS = ctx.enter_context(nc.psum_tensor("PS", [128, 8, 512], F32))

    def sb(self, ctx, name, shape, dt=F32):
        self.names += 1
        return ctx.enter_context(self.nc.sbuf_tensor(f"{name}_{self.names}", shape, dt))

    def dma(self, out, in_, *tokens):
        i = self.ndma % self.NSLOT
        self.ndma += 1
        self.sp.wait(self.landed[i])
        slot = self.slots[i]
        self.sp.wait(*tokens)
        self.sp.items.append(("do", lambda e: e.dma_start(out, in_).then_inc(slot, 16), Token(self.sp, len(self.sp.items))))
        self.landed[i] = Landed(slot, (self.landed[i].value if self.landed[i] else 0) + 16)
        return self.landed[i]

    def barrier(self):
        ends = [q.last for q in (self.pe, self.act, self.dve, self.pool)] + list(self.landed)
        for q in (self.pe, self.act, self.dve, self.pool, self.sp):
            q.wait(*[t for t in ends if not (isinstance(t, Token) and t.queue is q)])
        for q in (self.pe, self.act, self.dve, self.pool):
            q.wait(q.last)

    def emit(self):
        self.sp.wait(*self.landed)
        queues = (self.pe, self.act, self.dve, self.pool, self.sp)
        for q in queues:
            q.number()
        with self.nc.Block() as block:
            block.tensor(self.pe.emit)
            block.scalar(self.act.emit)
            block.vector(self.dve.emit)
            block.gpsimd(self.pool.emit)
            block.sync(self.sp.emit)


def view(t, off, dims, parts=None):
    base = t[:] if not isinstance(t, bass.AP) else t
    p = list(base.ap[0])
    if parts is not None:
        p[1] = parts
    return bass.AP(base.tensor, base.offset + off, [p] + [list(d) for d in dims])


def mm(out, lhsT, rhs, start=True, stop=True):
    return lambda e: e.matmul(out, lhsT, rhs, start=start, stop=stop)


def act(out, in_, fn, **kw):
    return lambda e: e.activation(out, in_, fn, **kw)


def tt(out, a, b, op):
    return lambda e: e.tensor_tensor(out, a, b, op)


def ts(out, a, s1, s2, op0, op1=ALU.bypass):
    if s2 is None:
        return lambda e: e.tensor_scalar(out, a, s1, None, op0)
    return lambda e: e.tensor_scalar(out, a, s1, s2, op0, op1)


def stt(out, a, s, b, op0, op1, **kw):
    return lambda e: e.scalar_tensor_tensor(out=out, in0=a, scalar=s, in1=b, op0=op0, op1=op1, **kw)


def copy(out, a):
    return lambda e: e.tensor_copy(out, a)


def groupnorm(P, K, g, x, bank, ready, scratch, small):
    s, m, v, r = (small[0:C, i:i + 1] for i in range(4))
    pm = P.PS[0:C, bank, 0:1]
    a = P.dve(lambda e: e.reduce_sum(s, x, axis=AX.X), ready)
    a = P.pe(mm(pm, g, s), a)
    a = P.dve(copy(m, pm), a)
    a = P.dve(ts(x, x, m, None, ALU.subtract), a)
    a = P.act(act(scratch, x, ACT.Square, accum_out=v), a)
    a = P.pe(mm(pm, g, v), a)
    a = P.act(act(r, pm, ACT.Sqrt, bias=K["eps5"][0:C, :]), a)
    a = P.dve(lambda e: e.reciprocal(s, r), a)
    return P.dve(ts(x, x, s, None, ALU.mult), a)



def attention(P, K, D, src, dst, scr):
    PS = P.PS
    KT = [(t * 128, min(128, L - t * 128)) for t in range(25)]
    scale = float(C) ** -0.5
    NQ, NPR, NG = 4, 5, 3 * NI
    with ExitStack() as ctx:
        sb = lambda n, s, d=F32: P.sb(ctx, n, s, d)
        wqk, wv = sb("wqk", [C, C]), sb("wv", [C, 48])
        wp, bp = sb("wp", [16, 3, C]), sb("bp", [C, 1])
        comb = sb("comb", [128, 32])
        xres, xg = sb("xres", [C, 2, L]), sb("xg", [C, L])
        parts = [sb(f"part{i}", [C, L], BF16) for i in range(3)]
        rem = sb("rem", [C, 2, T])
        Q = [sb(f"Q{h}", [99, L], BF16) for h in range(NQ)]
        KK = [sb(f"K{h}", [99, L], BF16) for h in range(NQ)]
        V = sb("V", [128, 2, 25, 3, 32])
        Pr = sb("Pr", [128, NPR, 2, T])
        ev = sb("ev", [128, 2, T])
        ost, rb = sb("ost", [32, 2, L]), sb("rb", [16, L])
        dn = sb("dn", [112, 28])
        oh = sb("oh", [16, 2, T])
        mx = sb("mx", [128, 25, 7])
        mr, mr2 = sb("mr", [128, 25]), sb("mr2", [128, 25])
        nm = sb("nm", [128, 25, 3], BF16)
        small = sb("small", [128, 8])
        w = [P.dma(t[:], D[k]) for t, k in ((wqk, "wqk"), (wv, "wv"), (wp, "wp"), (bp, "bp"), (comb, "comb"))]
        ones = [P.dve(lambda e, h=h: e.memset(KK[h][96:99, :], 1.0)) for h in range(NQ)]
        vinit = P.pool(lambda e: e.memset(V[:], 1.0))
        minit = P.dve(lambda e: e.memset(mx[:], 0.0))
        stacked, vready, mrow = {}, {}, {}
        gn, xfree, turned, stored = {}, {}, {}, {}
        got = {}
        free = {"b7": None, "mx": [None, None], "S": [None, None], "O": None, "ev": [None, None], "oh": [None, None],
                "rb": None, "dn": None, "nm": None, "tail": None}
        pfree = [None] * NPR

        def load(b):
            got[b] = P.dma(xres[:, b % 2, :], src[b], stored.get(b - 2))

        def load_g(b):
            got["g", b] = P.dma(xg[:], src[b], xfree.get(b - 1))

        def norm(b):
            x, v = xg[:], {}
            s_, m_, v_, r_ = (small[0:C, i:i + 1] for i in range(4))
            pm = PS[0:C, 7, 0:1]

            def put(key, fn):
                return lambda: v.__setitem__("a", fn(v.get("a")))

            def both(first):
                def f(a):
                    c = P.pe(mm(pm, K["gn"][:], s_ if first else v_), a, free["b7"])
                    if first:
                        free["b7"] = r = P.dve(copy(m_, pm), c)
                    else:
                        free["b7"] = r = P.act(act(r_, pm, ACT.Sqrt, bias=K["eps5"][0:C, :]), c)
                    return r
                return f

            steps = [put(0, lambda a: P.dve(lambda e: e.reduce_sum(s_, x, axis=AX.X), got["g", b], gn.get(b - 1))),
                     put(0, both(True)),
                     put(0, lambda a: P.dve(ts(x, x, m_, None, ALU.subtract), a)),
                     put(0, lambda a: P.act(act(parts[0][:], x, ACT.Square, accum_out=v_), a, turned.get(b - 1), gn.get(b - 1))),
                     put(0, both(False)),
                     put(0, lambda a: P.dve(lambda e: e.reciprocal(s_, r_), a)),
                     put(0, lambda a: P.dve(ts(x, x, s_, None, ALU.mult), a)),
                     lambda: gn.__setitem__(b, v["a"])]
            return steps

        def qkv(b):
            out, v = [], {}

            def c1(t):
                cols = slice(t * T, t * T + T)
                p = PS[0:C, 7, 0:T]
                a = P.pe(mm(p, wqk[:], xg[:, cols]), gn[b], w, free["b7"])
                hi = P.act(act(parts[0][:, cols], p, ACT.Copy), a, turned.get(b - 1))
                free["b7"] = v["r", t] = P.dve(tt(rem[:, t % 2, :], p, parts[0][:, cols], ALU.subtract),
                                               hi, v.get(("l", t - 2)))

            def c2(t):
                cols = slice(t * T, t * T + T)
                mid = P.act(act(parts[1][:, cols], rem[:, t % 2, :], ACT.Copy), v["r", t])
                v["l", t] = P.dve(tt(parts[2][:, cols], rem[:, t % 2, :], parts[1][:, cols], ALU.subtract), mid)
                v["m"] = [mid, v["l", t]]

            def vt(t):
                k0, kn = KT[t]
                p = PS[0:kn, 7, 0:48]
                a = P.pe(mm(p, xg[:, k0:k0 + kn], wv[:]), gn[b], w, free["b7"])
                xfree[b] = a
                free["b7"] = vready[b] = P.act(act(V[0:kn, b % 2, t, :, 0:16], p.rearrange("p (h d) -> p h d", h=3),
                                                   ACT.Copy), a, vinit, v["pv"])

            out += [lambda: v.__setitem__("pv", free["tail"])]
            for t in range(NT):
                out += [lambda t=t: c1(t), lambda t=t: c2(t)]
            out += [lambda: turned.__setitem__(("m", b), v["m"])]
            out += [lambda t=t: vt(t) for t in range(25)]
            return out

        def stack(g, tokens):
            b, h = divmod(g, 3)
            s = g % NQ
            stacked[g] = []
            for j, (a, c) in enumerate([(0, 0), (0, 1), (1, 0), (1, 1), (0, 2), (2, 0)]):
                rows = slice(16 * j, 16 * j + 16)
                stacked[g].append(P.dma(Q[s][rows, :], parts[a][16 * h:16 * h + 16, :], tokens, turned["m", b]))
                stacked[g].append(P.dma(KK[s][rows, :], parts[c][48 + 16 * h:64 + 16 * h, :], tokens, turned["m", b]))
            turned[b] = turned.get(b, []) + stacked[g]

        def maxima(g):
            s = g % NQ
            out, v = [], {}
            n = [0]

            def one(t, i):
                q0, qn = KT[t]
                m = n[0] % 2
                n[0] += 1
                a = P.pe(mm(PS[0:qn, 5 + m, 0:T], Q[s][0:96, q0:q0 + qn], KK[s][0:96, i * T:i * T + T]),
                         stacked[g], free["mx"][m])
                free["mx"][m] = P.dve(lambda e, o=mx[0:qn, t, i:i + 1], i_=PS[0:qn, 5 + m, 0:T]:
                                      e.tensor_reduce(o, i_, AX.X, ALU.max), a, minit, v.get("r"))

            def negative():
                a = P.dve(lambda e: e.tensor_reduce(mr[:], mx[:], AX.X, ALU.max), free["mx"])
                a = P.dve(ts(mr[:], mr[:], -1.0, None, ALU.mult), a)
                a = P.dve(copy(nm[:, :, 0], mr[:]), a, free["nm"])
                a = P.dve(tt(mr2[:], mr[:], nm[:, :, 0], ALU.subtract), a)
                a = P.dve(copy(nm[:, :, 1], mr2[:]), a)
                v["n"] = P.dve(tt(nm[:, :, 2], mr2[:], nm[:, :, 1], ALU.subtract), a)

            def rows(i):
                tiles = list(range(4 * i, min(4 * i + 4, 25)))
                n = 0
                for t in tiles:
                    kn = KT[t][1]
                    c = P.pe(mm(PS[0:3, 7, n:n + kn], nm[:, t, :], K["identb"][:, 0:kn]), v["n"], free["b7"])
                    n += kn
                q0 = KT[tiles[0]][0]
                free["nm"] = c
                free["b7"] = mrow[g] = P.act(act(Q[s][96:99, q0:q0 + n], PS[0:3, 7, 0:n], ACT.Copy), c)

            out += [lambda t=t, i=i: one(t, i) for t in range(25) for i in range(7)]
            return out + [negative] + [lambda i=i: rows(i) for i in range(7)]

        def finish(g):
            b, h = divmod(g, 3)
            o, v = ost[:, g % 2, :], {}
            d0, d1 = scr[2 * (g % 2)], scr[2 * (g % 2) + 1]

            def d():
                a = P.dma(d0, o[16:17, :], stored["o", g])
                v["d"] = P.dma(dn[:], d0.rearrange("a (p f) -> (a p) f", p=112), a, free["dn"])

            def r():
                a = P.dve(lambda e: e.reciprocal(dn[:], dn[:]), v["d"])
                free["dn"] = a = P.dma(d1.rearrange("a (p f) -> (a p) f", p=112), dn[:], a)
                v["b"] = P.dma(rb[:], d1.broadcast_to([16, L]), a, free["rb"])

            def m(qc):
                s, cols = qc % 2, slice(qc * T, qc * T + T)
                free["rb"] = v["m", qc] = P.dve(tt(oh[:, s, :], o[0:16, cols], rb[:, cols], ALU.mult), v["b"], free["oh"][s])
                stored["f", g] = v["m", qc]

            def p(qc):
                s, cols = qc % 2, slice(qc * T, qc * T + T)
                x = xres[:, b % 2, cols]
                free["oh"][s] = a = P.pe(mm(PS[0:C, 7, 0:T], wp[:, h, :], oh[:, s, :]), v["m", qc], w, free["b7"])
                if h == 0:
                    f = stt(x, PS[0:C, 7, 0:T], bp[:], x, ALU.add, ALU.add)
                else:
                    f = tt(x, PS[0:C, 7, 0:T], x, ALU.add)
                free["b7"] = a = P.dve(f, a, got[b], v.get("x"), stored.get(("x", b, qc)))
                stored["x", b, qc] = a
                if h == 2:
                    stored[b] = stored.get(b, []) + [P.dma(dst[b][:, cols], x, a)]

            out = [d] + [None] * 12 + [r] + [None] * 12
            for qc in range(NT):
                out += [lambda qc=qc: m(qc), lambda qc=qc: p(qc)]
            return out

        def run(steps):
            for f in steps:
                if f:
                    f()

        load_g(0)
        load(0)
        run(norm(0) + qkv(0))
        for g in range(3):
            stack(g, None)
        run(maxima(0))
        pvq, later = [], []
        n = 0
        tdone = {}

        def pv():
            g, qc, tiles, slot, ready = pvq.pop(0)
            b, h = divmod(g, 3)
            for i, t in enumerate(tiles):
                kn = KT[t][1]
                j = t % 4
                a = P.pe(mm(PS[32 * j:32 * j + 32, 4, 0:T], V[0:kn, b % 2, t, h, :], Pr[0:kn, slot, i, :],
                            start=(t < 4), stop=(t > 20)), ready, vready[b], free["O"] if t < 4 else None)
            pfree[slot] = free["tail"] = a
            if tiles[-1] == 24:
                s = qc % 2
                v = {}

                def e1():
                    free["O"] = v["e"] = P.act(act(ev[:, s, :], PS[:, 4, 0:T], ACT.Copy), a, free["ev"][s])

                def e2():
                    free["ev"][s] = v["c"] = P.pe(mm(PS[0:32, 7, 0:T], comb[:], ev[:, s, :]), v["e"], w, free["b7"])
                    free["b7"] = stored["o", g] = P.act(act(ost[:, g % 2, qc * T:qc * T + T], PS[0:32, 7, 0:T], ACT.Copy),
                                                        v["c"], stored.get(("f", g - 2)))

                e1()
                later.append((n + 1, e2))

        for g in range(NG):
            b, h = divmod(g, 3)
            s = g % NQ
            side = finish(g - 1) if g else []
            main = []
            if h == 0 and b + 1 < NI:
                load_g(b + 1)
            if h == 1 and b + 1 < NI:
                load(b + 1)
                main += norm(b + 1) + qkv(b + 1)
            if h == 2 and b + 1 < NI:
                stack(g + 3, tdone[g - 1])
            if g + 1 < NG:
                few, many = main, maxima(g + 1)
                main = []
                for i, f in enumerate(many):
                    main.append(f)
                    if few and i % 3 == 2:
                        main.append(few.pop(0))
                main += few
            if h == 1 and b + 1 < NI:
                main += [lambda: stack(3 * b + 3, tdone[3 * b - 1] if b else None), lambda: stack(3 * b + 4, tdone[3 * b])]
            slots, at = 7 * 13, 0
            for qc in range(NT):
                cols = slice(qc * T, qc * T + T)
                for pi in range(13):
                    tiles = list(range(2 * pi, min(2 * pi + 2, 25)))
                    m, slot = n % 2, n % NPR
                    kn = KT[tiles[0]][1]
                    at += 1
                    want = min(len(main) // (slots - at + 1) + 1 if slots > at else len(main), len(main))
                    for i, t in enumerate(tiles):
                        if i and want:
                            main.pop(0)()
                            want -= 1
                        k0 = KT[t][0]
                        a = P.pe(mm(PS[0:kn, 2 * m + i, 0:T], KK[s][0:99, k0:k0 + kn], Q[s][0:99, cols]),
                                 mrow[g], ones, free["S"][m])
                    free["S"][m] = P.act(act(Pr[0:kn, slot, 0:len(tiles), :], PS[0:kn, 2 * m:2 * m + len(tiles), 0:T],
                                             ACT.Exp, scale=scale), a, pfree[slot])
                    tdone[g] = a
                    pvq.append((g, qc, tiles, slot, free["S"][m]))
                    n += 1
                    while later and later[0][0] <= n:
                        later.pop(0)[1]()
                    if len(pvq) >= 4:
                        pv()
                    if side and at > 8:
                        f = side.pop(0)
                        if f:
                            f()
                    for _ in range(want):
                        main.pop(0)()
            while main:
                main.pop(0)()
        while pvq:
            n += 1
            pv()
            while later and later[0][0] <= n:
                later.pop(0)[1]()
        run([f for _, f in later])
        run(finish(NG - 1))
        P.barrier()



def pieces(order, j, w):
    j8 = 8 * j
    if order == 0:
        return [(j8 * w, [[w, 8], [1, 56]], 0, [[56, 8], [1, 56]])]
    if order == 1:
        return [(j8, [[1, 8], [w, 56]], 0, [[56, 8], [1, 56]])]
    step, n1 = (w + 1, 56 - j8) if order == 2 else (w - 1, j8 + 1)
    wrap = -56 if order == 2 else 56
    out = [(j8, [[1, 8], [step, n1]], 0, [[56, 8], [1, n1]])]
    if n1 < 56:
        out.append((j8 + wrap + n1 * step, [[1, 8], [step, 56 - n1]], n1, [[56, 8], [1, 56 - n1]]))
    return out


def run_dims(off, dims, rev):
    return (T - 1 - off, [[-s, n] for s, n in dims]) if rev else (off, dims)


class Layer:

    def __init__(self, pre, ratio, scans, width, dup):
        self.pre, self.ratio, self.scans, self.width, self.dup = pre, ratio, scans, width, dup


L1 = Layer("l1", False, [(0, False), (1, False), (0, True), (1, True), (2, False), (3, False), (2, True), (3, True)], 64, 8)
L3 = Layer("l3", True, [(0, False), (0, True), (1, False), (1, True)], 56, 0)


VT = [(0, 1, 2, 3, 5), (0, 1, 2, 3, 5), (0, 1, 3, 5)]


def edges(P, pad):
    P.pool(lambda e: e.memset(view(pad, 0, [[58 * 58, 3], [57 * 58, 2], [1, 58]]), 0.0))
    return P.pool(lambda e: e.memset(view(pad, 58, [[58 * 58, 3], [58, 56], [57, 2]]), 0.0))


def halves(P, w, src):
    z = P.dve(lambda e: e.memset(w[:], 0.0))
    return [P.dma(w[64 * i:64 * i + 64, i], src[64 * i:64 * i + 64], z) for i in range(2)]


def taps(P, acc, pad, cw, c, t, *tokens):
    o = acc.rearrange("p (a b) -> p a b", b=56)
    for k in range(9):
        dy, dx = k // 3, k % 3
        x = pad[:, c, 8 * t + dy:8 * t + dy + 8, dx:dx + 56]
        if k == 0:
            a = P.dve(ts(o, x, cw[:, c, 0:1], None, ALU.mult), *tokens)
        else:
            a = P.dve(stt(o, x, cw[:, c, k:k + 1], o, ALU.mult, ALU.add), a)
    return a


def front(P, K, D, lay, pair, src, xc, zd):
    PS, pre = P.PS, lay.pre
    w = lay.width
    with ExitStack() as ctx:
        sb = lambda n, s, d=F32: P.sb(ctx, n, s, d)
        win = sb("win", [C, 384])
        cw, cb = sb("cw", [128, 3, 9]), sb("cb", [128, 3])
        diag = sb("diag", [128, 3, 9, 128])
        xg = [sb(f"xg{i}", [C, L]) for i in range(2)]
        pad = sb("pad", [128, 3, 58, 58])
        zst = sb("zst", [128, 3, T])
        acc = sb("acc", [128, 6, T])
        junk = sb("junk", [C, L], BF16)
        small = sb("small", [128, 8])
        lw = [P.dma(win[:], D[pre + "win"]), P.dma(cw[:], D[pre + "cw"]), P.dma(cb[:], D[pre + "cb"])]
        z0 = edges(P, pad)
        ld = [P.dma(xg[i][:], src[2 * pair + i]) for i in range(2)]
        dg = None
        for c in range(3):
            for k in range(9):
                dg = P.pool(ts(diag[:, c, k, :], K["ident"][:], cw[:, c, k:k + 1], None, ALU.mult), lw)
        gn = []
        for i in range(2):
            gn.append(groupnorm(P, K, K["gn"][:], xg[i][:], 7, [ld[i], P.pe.last, gn[-1:]], junk[:], small))
        free = [None] * 4
        n = 0
        zout = [None] * 3
        for c0 in (0, 3):
            for t, c in ((t, c) for t in range(NT) for c in range(c0, c0 + 3)):
                s = n % 4
                n += 1
                for i in range(2):
                    a = P.pe(mm(PS[64 * i:64 * i + 64, s, 0:T], win[:, 64 * c:64 * c + 64], xg[i][:, t * T:t * T + T]),
                             gn, lw, free[s])
                if c < 3:
                    free[s] = inpad = P.act(act(pad[:, c, 1 + 8 * t:9 + 8 * t, 1:57],
                                                PS[:, s, 0:T].rearrange("p (a b) -> p a b", b=56), ACT.Copy), a, z0)
                else:
                    fn = ACT.Copy if lay.ratio else ACT.Silu
                    free[s] = a = P.act(act(zst[:, c - 3, :], PS[:, s, 0:T], fn), a, zout[c - 3])
                    zout[c - 3] = P.dma(zd[pair, :, c - 3, t * T:t * T + T], zst[:, c - 3, :], a)
        afree = [None] * 6
        nv = 0
        for c in range(3):
            for t in (0, 2, 1, 4, 3, 6, 5):
                o = view(xc, c * H * w + 8 * t * w, [[w, 8], [1, 56]])
                if t in VT[c]:
                    v = nv % 6
                    nv += 1
                    a = taps(P, acc[:, v, :], pad, cw, c, t, inpad, lw, afree[v])
                    afree[v] = a = P.act(act(o, acc[:, v, :].rearrange("p (a b) -> p a b", b=56), ACT.Silu,
                                             bias=cb[:, c:c + 1]), a)
                    continue
                s = n % 4
                n += 1
                for k in range(9):
                    dy, dx = k // 3, k % 3
                    a = P.pe(mm(PS[:, s, 0:T], diag[:, c, k, :], pad[:, c, 8 * t + dy:8 * t + dy + 8, dx:dx + 56],
                                start=(k == 0), stop=(k == 8)), inpad, dg, free[s])
                free[s] = a = P.act(act(o, PS[:, s, 0:T].rearrange("p (a b) -> p a b", b=56), ACT.Silu,
                                        bias=cb[:, c:c + 1]), a)
            if lay.dup:
                P.pool(copy(view(xc, c * H * w + 56, [[w, 56], [1, 8]]), view(xc, c * H * w, [[w, 56], [1, 8]])), a)
        P.barrier()


def scans(P, K, D, lay, pair, xc, yacc):
    PS, pre, w = P.PS, lay.pre, lay.width
    NK = len(lay.scans)
    ratio = lay.ratio
    if ratio:
        BA, BW, BC, BY, BX = [0, 1], [2, 3], [4, 5], [6], [7]
    else:
        BA, BC, BY, BX = [0, 1, 2], [3, 4], [5, 6], [7]
    with ExitStack() as ctx:
        sb = lambda n, s, d=F32: P.sb(ctx, n, s, d)
        xp = sb("xp", [128, 2, 3, 76])
        dw = sb("dw", [12, 2, 3, 128])
        A = sb("A", [128, NK, 3, 16])
        db = sb("db", [128, NK, 3])
        ds = sb("ds", [128, 3, NK])
        dsum = sb("dsum", [128, 3])
        xs, dl, du = sb("xs", [128, 2, 3, T]), sb("dl", [128, 2, 3, T]), sb("du", [128, 2, 3, T])
        if ratio:
            cs = sb("cs", [128, 2, 3, T])
            one = K["one"][:, 0:1].broadcast_to([128, T])
            A2 = sb("A2", [128, NK, 3, 16])
            NT2 = 2
            T2 = sb("T2", [128, NT2, T])
            Wr = sb("Wr", [128, T])
        dts = sb("dts", [12, T])
        lg, w1 = sb("lg", [128, 3, T]), sb("w1", [128, 3, T])
        SB_, SC = sb("SB", [C, T], BF16), sb("SC", [C, 2, T], BF16)
        part = sb("part", [64, 3, T], BF16)
        rt = sb("rt", [64, T])
        Bs = sb("Bs", [128, 16, T])
        NTR, NH, NHC = (4, 8, 3) if ratio else (4, 8, 4)
        Tr, Hr, Hc = sb("Tr", [128, NTR, T]), sb("Hr", [128, NH, T]), sb("Hc", [128, NHC, T])
        st = sb("st", [128, 48])

        ld = [P.dma(A[:], D[pre + "A"]), P.dma(db[:], D[pre + "db"]), P.dma(ds[:], D[pre + "ds"])]
        la = ld
        if not ratio:
            a = P.act(act(A[:], A[:], ACT.Exp), ld)
            la = a = P.dve(ts(A[:], A[:], -1.0, None, ALU.mult), a)
        else:
            a = P.dve(ts(A2[:], A[:], 0.5, None, ALU.mult), ld)
            a = P.dve(ts(A[:], A[:], -1.0, None, ALU.mult), a)
            la = P.dve(ts(A2[:], A2[:], -1.0, None, ALU.mult), a)
        a = P.dve(lambda e: e.reduce_sum(dsum[:], ds[:], axis=AX.X), ld)
        n = H * w
        for c in range(3):
            if ratio:
                z = P.dve(lambda e, c=c: e.memset(yacc[:, c * n:(c + 1) * n], 0.0), a)
                ini = P.dve(ts(yacc[:, c * n:(c + 1) * n], yacc[:, c * n:(c + 1) * n], dsum[:, c:c + 1], None, ALU.add), z)
            else:
                ini = P.dve(ts(yacc[:, c * n:(c + 1) * n], xc[:, c * n:(c + 1) * n], dsum[:, c:c + 1], None, ALU.mult), a)
        if lay.dup:
            ini = P.dve(lambda e: e.memset(view(yacc, 56, [[w, 3 * H], [1, w - 56]]), 0.0), ini)

        NC_ = NK * NT
        NU = NC_ * 48
        tA, tC, tT, tS, tH, tY, tW, tT2 = ([None] * NU for _ in range(8))
        dlready, duready, csready = [None] * NC_, [None] * NC_, [None] * NC_
        scready, sbready, wld = [None] * NC_, [None] * NC_, [None] * NK
        bready = {}
        free = dict.fromkeys(("bx", "dts", "part", "rt", "SB", "lg", "w1"))
        carry = {}
        yev = {}
        yevlast = [ini]
        XB = PS[:, BX[0], 0:T]
        SHARE = 4
        half = 0.5 if ratio else 1.0

        def load(k):
            s = k % 2
            wld[k] = [P.dma(xp[:, s], D[pre + "xp"][k], P.pe.last), P.dma(dw[:, s], D[pre + "dw"][k], P.pe.last)]

        def steps(q):
            k, j = divmod(q, NT)
            order, rev = lay.scans[k]
            jj = NT - 1 - j if rev else j
            s, ks = q % 2, k % 2
            X = xs[:, s]
            if j == 0:
                load(k)
            old = [t[48 * (q - 1) - 1] for t in (tA, tT, tW)] if q >= 2 else []
            oldc = tC[48 * (q - 1) - 1] if q >= 2 else None
            v = {}
            out = []

            def gather(p, c):
                off, dims, ro, rd = p
                ro, rd = run_dims(ro, rd, rev)
                v["g"] = P.act(act(view(xs, (s * 3 + c) * T + ro, rd), view(xc, c * n + off, dims), ACT.Copy),
                               duready[q - 2] if q >= 2 else None, v.get("x"))

            def proj(c):
                v["p"] = P.pe(mm(PS[0:76, BX[0], 0:T], xp[:, ks, c, :], X[:, c, :], start=(c == 0), stop=(c == 2)),
                              v["g"], wld[k], free["bx"])

            def high():
                v["dts"] = P.act(act(dts[:], PS[64:76, BX[0], 0:T], ACT.Copy), v["p"], free["dts"])
                v["h"] = P.act(act(part[:, 0, :], PS[0:64, BX[0], 0:T], ACT.Copy), v["p"], free["part"])

            def rest():
                free["bx"] = v["r"] = P.dve(tt(rt[:], PS[0:64, BX[0], 0:T], part[:, 0, :], ALU.subtract),
                                            v["h"], free["rt"])

            def middle():
                v["m"] = P.act(act(part[:, 1, :], rt[:], ACT.Copy), v["r"])

            def low():
                free["rt"] = v["l"] = P.dve(tt(part[:, 2, :], rt[:], part[:, 1, :], ALU.subtract), v["m"])

            def place():
                moved = [[], []]
                for i in range(3):
                    moved[0].append(P.dma(SB_[32 * i:32 * i + 32, :], part[0:32, i, :], v["l"], v["m"], free["SB"]))
                    moved[1].append(P.dma(SC[32 * i:32 * i + 32, s, :], part[32:64, i, :], v["l"], v["m"], oldc))
                sbready[q], scready[q] = moved
                free["part"] = moved[0] + moved[1]

            def pre_delta(c):
                v["x"] = free["dts"] = P.pe(mm(XB, dw[:, ks, c, :], dts[:]), v["dts"], wld[k], free["bx"])

            def absolute(c):
                P.act(act(du[:, s, c, :], XB, ACT.Abs, bias=db[:, k, c:c + 1]), v["x"], ld, old)
                free["bx"] = v["a"] = P.act(act(dl[:, s, c, :], XB, ACT.Relu, bias=db[:, k, c:c + 1]))

            def expo(c):
                v["e"] = P.act(act(du[:, s, c, :], du[:, s, c, :], ACT.Exp, scale=-1.0), v["a"])

            def loga(c):
                v["l"] = P.act(act(lg[:, c, :], du[:, s, c, :], ACT.Ln, bias=K["one"][:]), v["e"], free["lg"])

            def minus_w(c):
                if ratio:
                    v["w"] = P.pool(ts(w1[:, c, :], du[:, s, c, :], -1.0, -1.0, ALU.mult, ALU.add), v["e"], free["w1"])
                    return
                v["w"] = P.act(act(w1[:, c, :], du[:, s, c, :], ACT.Identity, scale=-1.0, bias=K["mone"][:]), v["e"], free["w1"])

            def correction():
                v["c"] = P.dve(stt(w1[:], w1[:], 1.0, du[:, s], ALU.add, ALU.add), v["w"])

            def total(c):
                if not ratio:
                    v["s"] = P.dve(tt(lg[:, c, :], lg[:, c, :], dl[:, s, c, :], ALU.add), v["l"])
                    free["lg"] = free["w1"] = dlready[q] = P.dve(tt(dl[:, s, c, :], lg[:, c, :], w1[:, c, :], ALU.add),
                                                                 v["s"], v["c"])
                    return
                P.pe(mm(XB, K["ident"][:], dl[:, s, c, :], stop=False), v["l"], free["bx"])
                P.pe(mm(XB, K["ident"][:], lg[:, c, :], start=False, stop=False))
                free["lg"] = free["w1"] = v["t"] = P.pe(mm(XB, K["ident"][:], w1[:, c, :], start=False), v["c"])

            def delta(c):
                free["bx"] = dlready[q] = v["d", c] = P.act(act(dl[:, s, c, :], XB, ACT.Copy), v["t"])

            def inputs(c):
                duready[q] = P.pool(tt(du[:, s, c, :], dl[:, s, c, :], X[:, c, :], ALU.mult), v.get(("d", c), dlready[q]))

            def cumsum(c):
                init = 0.0 if j == 0 else cs[:, 1 - s, c, T - 1:T]
                csready[q] = P.dve(lambda e: e.tensor_tensor_scan(cs[:, s, c, :], one, dl[:, s, c, :], init,
                                                                 ALU.mult, ALU.add),
                                   v["d", c], csready[q - 1] if q else None, old, la)

            out = [lambda p=p, c=c: gather(p, c) for c in range(3) for p in pieces(order, jj, w)]
            out += [lambda c=c: proj(c) for c in range(3)]
            out += [high, rest, middle, low, place]
            out += [f for c in range(3) for f in (lambda c=c: pre_delta(c), lambda c=c: absolute(c))]
            if ratio:
                out += [lambda c=c: expo(c) for c in range(3)] + [lambda: [loga(c) for c in range(3)]]
                out += [lambda c=c: minus_w(c) for c in range(3)] + [correction]
                both = lambda f, g, c, d: lambda: (f(c), g(d))
                out += [lambda: total(0), lambda: delta(0), both(total, inputs, 1, 0), both(delta, cumsum, 1, 0),
                        both(total, inputs, 2, 1), both(delta, cumsum, 2, 1), lambda: inputs(2), lambda: cumsum(2)]
            else:
                out += [f for c in range(3) for f in (lambda c=c: expo(c), lambda c=c: loga(c))]
                out += [lambda c=c: minus_w(c) for c in range(3)] + [correction]
                out += [lambda c=c: total(c) for c in range(3)] + [lambda c=c: inputs(c) for c in range(3)]
            return out

        def bc_mm(q, nn):
            free["SB"] = P.pe(mm(XB, K["sel"][:, nn, :], SB_[:]), sbready[q], free["bx"])

        def bc_copy(q, nn):
            free["bx"] = bready[(q, nn)] = P.act(act(Bs[:, nn, :], XB, ACT.Copy, scale=half), free["SB"],
                                                 tT[48 * (q - 1) + 32 + nn] if q else None)

        def pooled(i):
            return ratio and i % SHARE == SHARE - 1

        mine = [i for i in range(NU) if not pooled(i)]
        before = dict(zip(mine, [None, None] + mine))

        def slot2(i):
            return (i - (i + 1) // SHARE) % NT2

        def uT(i):
            q, r = divmod(i, 48)
            c, nn = divmod(r, 16)
            tT[i] = P.pool(tt(Tr[:, i % NTR, :], du[:, q % 2, c, :], Bs[:, nn, :], ALU.mult),
                           duready[q], bready[(q, nn)], (tT2 if ratio and not pooled(i - NTR) else tS)[i - NTR] if i >= NTR else None)

        def uA(i):
            q, r = divmod(i, 48)
            c, nn = divmod(r, 16)
            k = q // NT
            tA[i] = P.act(act(PS[:, BA[i % len(BA)], 0:T], dl[:, q % 2, c, :], ACT.Exp, scale=A[:, k, c, nn:nn + 1]),
                          dlready[q], la, tS[i - len(BA)] if i >= len(BA) else None)

        def uW(i):
            q, r = divmod(i, 48)
            c, nn = divmod(r, 16)
            k = q // NT
            o, last = (Wr[:], i - SHARE) if pooled(i) else (PS[:, BW[slot2(i)], 0:T], before[i])
            tW[i] = P.act(act(o, cs[:, q % 2, c, :], ACT.Tanh, scale=A2[:, k, c, nn:nn + 1],
                              bias=K["lneps"][:]), csready[q], la, None if last is None or last < 0 else tT2[last])
            if pooled(i):
                tW[i] = P.act(act(o, o, ACT.Identity, bias=K["one"][:]), tW[i])

        def uT2(i):
            if pooled(i):
                t = Tr[:, i % NTR, :]
                tT2[i] = P.pool(tt(t, Wr[:], t, ALU.mult), tW[i], tT[i])
                return
            tT2[i] = P.dve(stt(T2[:, slot2(i), :], PS[:, BW[slot2(i)], 0:T], 1.0, Tr[:, i % NTR, :], ALU.add, ALU.mult),
                           tW[i], tT[i], None if before[i] is None else tS[before[i]])

        def uC(i):
            q, r = divmod(i, 48)
            nn = r % 16
            tC[i] = P.pe(mm(PS[:, BC[i % 2], 0:T], K["sel"][:, nn, :], SC[:, q % 2, :]),
                         scready[q], tH[i - 2] if i >= 2 else None)

        def uS(i):
            q, r = divmod(i, 48)
            j = q % NT
            init = 0.0 if j == 0 else st[:, r:r + 1]
            inp = T2[:, slot2(i), :] if ratio and not pooled(i) else Tr[:, i % NTR, :]
            tS[i] = P.dve(lambda e: e.tensor_tensor_scan(Hr[:, i % NH, :], PS[:, BA[i % len(BA)], 0:T], inp, init,
                                                         ALU.mult, ALU.add),
                          tA[i], tT2[i] if ratio else tT[i], tH[i - NH] if i >= NH else None,
                          carry.get((q - 1, r // 4)) if j else None, carry.get(divmod(i - NH, 48)[0:1] + (((i - NH) % 48) // 4,)))
            if i % 4 == 3:
                carry[(q, r // 4)] = P.act(act(st[:, r - 3:r + 1], view(Hr, (i - 3) % NH * T + T - 1, [[T, 4]]), ACT.Copy), tS[i])

        def uH(i):
            tH[i] = P.dve(tt(Hc[:, i % NHC, :], PS[:, BC[i % 2], 0:T], Hr[:, i % NH, :], ALU.mult),
                          tS[i], tC[i], tY[i - NHC] if i >= NHC else None)

        def uY(i):
            q, r = divmod(i, 48)
            c, nn = divmod(r, 16)
            g = 3 * q + c
            tY[i] = P.pe(mm(PS[:, BY[g % len(BY)], 0:T], K["ident"][:], Hc[:, i % NHC, :], start=(nn == 0), stop=(nn == 15)),
                         tH[i], yev.get(g - len(BY)) if nn == 0 else None)

        def uE(g):
            q, c = divmod(g, 3)
            k, j = divmod(q, NT)
            order, rev = lay.scans[k]
            jj = NT - 1 - j if rev else j
            for off, dims, ro, rd in pieces(order, jj, w):
                ro, rd = run_dims(ro, rd, rev)
                o = view(yacc, c * n + off, dims)
                i_ = view(PS[:, BY[g % len(BY)], :], ro, rd)
                a = P.dve(tt(o, i_, o, ALU.add), tY[16 * g + 15], yevlast[0])
            yevlast[0] = yev[g] = a

        if not ratio:
            P.act.wait(*[q.last for q in (P.pe, P.dve, P.pool)])
            P.act(lambda e: e.preload_act_table_set("natural_log_exp_and_others"))
        for f in steps(0):
            f()
        for nn in range(16):
            bc_mm(0, nn)
            bc_copy(0, nn)
        ahead = len(BA) - 1
        for i in range(2):
            uT(i)
        for i in range(ahead):
            uA(i)
        if ratio:
            uW(0)
            uW(1)
            uT2(0)
        uC(0)
        pend, todo = [], []
        for i in range(NU):
            q, r = divmod(i, 48)
            if r == 0:
                todo = steps(q + 1) if q + 1 < NC_ else []
                total, done = len(todo), 0
            if i + 2 < NU:
                uT(i + 2)
            if i + ahead < NU:
                uA(i + ahead)
            if ratio:
                if i + 1 < NU:
                    uT2(i + 1)
                if i + 2 < NU:
                    uW(i + 2)
            while todo and done < total * (r + 1) / 31:
                todo.pop(0)()
                done += 1
            uS(i)
            if i >= 1:
                uH(i - 1)
                if i + 1 < NU:
                    uC(i + 1)
                if pend and pend[0][0] <= i:
                    uE(pend.pop(0)[1])
                if i >= 2:
                    uY(i - 2)
                if i >= 17 and (i - 2) % 16 == 15:
                    pend.append((i + 1 if ratio else i + 2, (i - 2) // 16))
            elif i + 1 < NU:
                uC(i + 1)
            if r >= 32 and q + 1 < NC_:
                bc_copy(q + 1, r - 32)
            if 31 <= r < 47 and q + 1 < NC_:
                bc_mm(q + 1, r - 31)
        uH(NU - 1)
        uY(NU - 2)
        uY(NU - 1)
        for _, g in pend:
            uE(g)
        uE(NU // 16 - 1)
        P.barrier()
        if lay.dup:
            a = P.dve(tt(view(yacc, 0, [[w, 3 * H], [1, 8]]), view(yacc, 0, [[w, 3 * H], [1, 8]]),
                         view(yacc, 56, [[w, 3 * H], [1, 8]]), ALU.add))
            P.barrier()


def tail_norm(P, K, sb, yacc, w):
    PS = P.PS
    rstd = sb("rstd", [128, L])
    sq = sb("sq", [128, 2, 3, T])
    sd = sb("sd", [128, 2, T])
    free, vfree, sqfree = [None, None], [None, None], [None, None]
    n = H * w

    def centre(t):
        s = t % 2
        for c in range(3):
            a = P.pe(mm(PS[:, s, 0:T], K["blk"][:], view(yacc, c * n + 8 * t * w, [[w, 8], [1, 56]]),
                        start=(c == 0), stop=(c == 2)), free[s])
        for c in range(3):
            yc = view(yacc, c * n + 8 * t * w, [[w, 8], [1, 56]])
            a = P.dve(tt(yc, yc, PS[:, s, 0:T].rearrange("p (a b) -> p a b", b=56), ALU.subtract), a)
        free[s] = a
        for c in range(3):
            a2 = P.act(act(sq[:, s, c, :].rearrange("p (a b) -> p a b", b=56),
                           view(yacc, c * n + 8 * t * w, [[w, 8], [1, 56]]), ACT.Square), a, sqfree[s])
        squared[t] = a2

    def deviation(t):
        s = t % 2
        for c in range(3):
            a = P.pe(mm(PS[:, 2 + s, 0:T], K["blk"][:], sq[:, s, c, :], start=(c == 0), stop=(c == 2)), squared[t], vfree[s])
        sqfree[s] = a
        a = P.act(act(sd[:, s, :], PS[:, 2 + s, 0:T], ACT.Sqrt, bias=K["eps5"][:]), a, vfree[s])
        vfree[s] = P.dve(lambda e: e.reciprocal(rstd[:, t * T:t * T + T], sd[:, s, :]), a)

    squared = {}
    for t in range(NT + 1):
        if t < NT:
            centre(t)
        if t:
            deviation(t - 1)
    return rstd, vfree[(NT - 1) % 2]


def gated(P, K, sb, ctx_ld, zd, pair, yacc, w, rstd, ready, lg, lb):
    z = sb("z", [128, 2, 3, T])
    zfree = [None, None]
    n = H * w
    out = []
    for t in range(NT):
        s = t % 2
        lz = P.dma(z[:, s], zd[pair, :, :, t * T:t * T + T], zfree[s])
        for c in range(3):
            yc = view(yacc, c * n + 8 * t * w, [[w, 8], [1, 56]])
            r = rstd[:, t * T:t * T + T].rearrange("p (a b) -> p a b", b=56)
            a = P.dve(stt(yc, yc, lg[:, c:c + 1], r, ALU.mult, ALU.mult), ready, ctx_ld)
            a = P.dve(stt(yc, yc, lb[:, c:c + 1], z[:, s, c, :].rearrange("p (a b) -> p a b", b=56), ALU.add, ALU.mult),
                      a, lz)
        zfree[s] = a
        out.append(a)
    return out


def tail1(P, K, D, pair, src, dst, yacc, zd):
    PS, w = P.PS, L1.width
    with ExitStack() as ctx:
        sb = lambda n, s, d=F32: P.sb(ctx, n, s, d)
        wo, lg, lb = sb("wo", [128, 2, 3, C]), sb("lg", [128, 3]), sb("lb", [128, 3])
        ld = [*halves(P, wo, D["l1wo"]), P.dma(lg[:], D["l1lg"]), P.dma(lb[:], D["l1lb"])]
        rstd, r = tail_norm(P, K, sb, yacc, w)
        g = gated(P, K, sb, ld, zd, pair, yacc, w, rstd, r, lg, lb)
        xr, yo = sb("xr", [C, 4, T]), sb("yo", [C, 4, T])
        free, bfree = [None] * 4, [None] * 2
        n = H * w
        for t in range(NT):
            for i in range(2):
                u = 2 * t + i
                s = u % 4
                img, cols = 2 * pair + i, slice(t * T, t * T + T)
                lx = P.dma(xr[:, s, :], src[img][:, cols], free[s])
                p = PS[0:C, 4 + u % 2, 0:T]
                for c in range(3):
                    rhs = view(yacc, c * n + 8 * t * w, [[w, 8], [1, 56]])
                    a = P.pe(mm(p, wo[:, i, c, :], rhs, start=(c == 0), stop=(c == 2)),
                             g[t], ld, bfree[u % 2])
                bfree[u % 2] = a = P.dve(tt(yo[:, s, :], p, xr[:, s, :], ALU.add), a, lx, free[s])
                free[s] = P.dma(dst[img][:, cols], yo[:, s, :], a)
        P.barrier()


def bnfold(P, K, sb, name, D, key, bias, n, waits):
    t = sb(name, [128, 4, n])
    o = sb(name + "o", [128, 2, n])
    ld = [P.dma(t[:], D[key]), waits]
    a = P.act(act(o[:, 0], t[:, 3], ACT.Sqrt, bias=K["eps5"][:]), ld)
    a = P.dve(lambda e: e.reciprocal(o[:, 1], o[:, 0]), a)
    a = P.dve(tt(o[:, 0], o[:, 1], t[:, 0], ALU.mult), a)
    b = P.dve(tt(o[:, 1], bias, t[:, 2], ALU.subtract), a)
    b = P.dve(tt(o[:, 1], o[:, 1], o[:, 0], ALU.mult), b)
    b = P.dve(tt(o[:, 1], o[:, 1], t[:, 1], ALU.add), b)
    return o, b


def tail3(P, K, D, pair, src, dst, yacc, zd):
    PS, w = P.PS, L3.width
    n = H * w
    with ExitStack() as ctx:
        sb = lambda n, s, d=F32: P.sb(ctx, n, s, d)
        lg, lb = sb("lg", [128, 3]), sb("lb", [128, 3])
        b1, b2 = sb("b1", [128, 3]), sb("b2", [128, 3])
        ld = [P.dma(lg[:], D["l3lg"]), P.dma(lb[:], D["l3lb"]), P.dma(b1[:], D["c1b"]), P.dma(b2[:], D["c2b"])]
        bn1, t1 = bnfold(P, K, sb, "bn1", D, "bn1", b1[:], 3, ld)
        bn2, t2 = bnfold(P, K, sb, "bn2", D, "bn2", b2[:], 3, ld)
        with ExitStack() as c2:
            sb2 = lambda n, s, d=F32: P.sb(c2, n, s, d)
            rstd, r = tail_norm(P, K, sb2, yacc, w)
            gated(P, K, sb2, ld, zd, pair, yacc, w, rstd, r, lg, lb)
            P.barrier()
        w1, cw, w3 = sb("w1", [128, 2, 3, 384]), sb("cw", [128, 3, 9]), sb("w3", [128, 3, C])
        diag = sb("diag", [128, 3, 9, 128])
        c3b, s1w, s1b = sb("c3b", [C, 1]), sb("s1w", [C, 48]), sb("s1b", [48, 1])
        s2w, s2b = sb("s2w", [48, C]), sb("s2b", [C, 1])
        pad = sb("pad", [128, 3, 58, 58])
        cv = sb("cv", [128, 2, 3, T])
        acc = sb("acc", [128, 2, T])
        t3 = sb("t3", [C, L])
        xr = sb("xr", [C, L])
        sums, sm, s1, s2 = sb("sums", [C, NT]), sb("sm", [C, 1]), sb("s1", [48, 1]), sb("s2", [C, 1])
        lw = [*halves(P, w1, D["c1w"]), P.dma(cw[:], D["c2w"]), P.dma(w3[:], D["c3w"]), P.dma(c3b[:], D["c3b"]),
              P.dma(s1w[:], D["s1w"]), P.dma(s1b[:], D["s1b"]), P.dma(s2w[:], D["s2w"]), P.dma(s2b[:], D["s2b"])]
        z0 = edges(P, pad)
        for c in range(3):
            for k in range(9):
                dg = P.pool(ts(diag[:, c, k, :], K["ident"][:], cw[:, c, k:k + 1], None, ALU.mult), lw)
        out = None
        afree = [None, None]
        for i in range(2):
            img = 2 * pair + i
            lx = P.dma(xr[:], src[img], out)
            free = [None] * 4
            u = 0
            for c in range(3):
                for t in range(NT):
                    s = u % 4
                    u += 1
                    for cc in range(3):
                        rhs = view(yacc, cc * n + 8 * t * w, [[w, 8], [1, 56]])
                        a = P.pe(mm(PS[:, s, 0:T], w1[:, i, cc, 128 * c:128 * c + 128], rhs,
                                    start=(cc == 0), stop=(cc == 2)), lw, free[s])
                    free[s] = inpad = P.act(act(pad[:, c, 1 + 8 * t:9 + 8 * t, 1:57],
                                                PS[:, s, 0:T].rearrange("p (a b) -> p a b", b=56), ACT.Relu,
                                                scale=bn1[:, 0, c:c + 1], bias=bn1[:, 1, c:c + 1]), a, z0, t1, P.pe.last)
            cvfree, ofree, ready = [None] * 2, [None] * 2, {}

            def conv(t):
                v, s = t % 2, t % 4
                for k in range(9):
                    dy, dx = k // 3, k % 3
                    a = P.pe(mm(PS[:, s, 0:T], diag[:, 2, k, :], pad[:, 2, 8 * t + dy:8 * t + dy + 8, dx:dx + 56],
                                start=(k == 0), stop=(k == 8)), inpad, dg, free[s])
                sums_ = [taps(P, acc[:, c, :], pad, cw, c, t, inpad, lw, afree[c]) for c in range(2)]
                free[s] = P.act(act(cv[:, v, 2, :], PS[:, s, 0:T], ACT.Relu,
                                    scale=bn2[:, 0, 2:3], bias=bn2[:, 1, 2:3]), a, t2, cvfree[v])
                for c in range(2):
                    afree[c] = P.act(act(cv[:, v, c, :], acc[:, c, :], ACT.Relu,
                                         scale=bn2[:, 0, c:c + 1], bias=bn2[:, 1, c:c + 1]), sums_[c])
                ready[t] = afree[1]

            def reduce_(t):
                v = t % 2
                p = PS[0:C, 4 + v, 0:T]
                for c in range(3):
                    a = P.pe(mm(p, w3[:, c, :], cv[:, v, c, :], start=(c == 0), stop=(c == 2)), ready[t], ofree[v])
                cvfree[v] = a
                ofree[v] = P.act(act(t3[:, t * T:t * T + T], p, ACT.Identity, bias=c3b[:],
                                     accum_out=sums[:, t:t + 1]), a, out)

            for t in range(NT + 1):
                if t < NT:
                    conv(t)
                if t:
                    reduce_(t - 1)
            a = ofree[(NT - 1) % 2]
            a = P.dve(lambda e: e.reduce_sum(sm[:], sums[:], axis=AX.X), a, P.act.last)
            b = P.pe(mm(PS[0:48, 6, 0:1], s1w[:], sm[:]), a)
            a = P.act(act(s1[:], PS[0:48, 6, 0:1], ACT.Relu, bias=s1b[:], scale=1.0 / L), b)
            b = P.pe(mm(PS[0:C, 7, 0:1], s2w[:], s1[:]), a)
            a = P.act(act(s2[:], PS[0:C, 7, 0:1], ACT.Sigmoid, bias=s2b[:]), b)
            a = P.dve(ts(s2[:], s2[:], 1.0, None, ALU.add), a)
            a = P.dve(stt(xr[:], t3[:], s2[:], xr[:], ALU.mult, ALU.add), a, lx)
            out = P.dma(dst[img], xr[:], a)
        P.barrier()


def ssm(P, K, D, lay, src, dst, zd):
    w = lay.width
    for pair in range(2):
        with ExitStack() as ctx:
            yacc = P.sb(ctx, "yacc", [128, 3 * H * w])
            with ExitStack() as c2:
                xc = P.sb(c2, "xc", [128, 3 * H * w])
                front(P, K, D, lay, pair, src, xc, zd)
                scans(P, K, D, lay, pair, xc, yacc)
            (tail3 if lay.ratio else tail1)(P, K, D, pair, src, dst, yacc, zd)



def local(P, K, D, src, dst):
    PS = P.PS
    with ExitStack() as ctx:
        sb = lambda n, s, d=F32: P.sb(ctx, n, s, d)
        w1, b1, w2, b2 = sb("w1", [C, 192]), sb("b1", [C, 2]), sb("w2", [C, 2, C]), sb("b2", [C, 1])
        lg, lb = sb("lg", [C, 1]), sb("lb", [C, 1])
        mask = sb("mask", [112, 30 * 56])
        xres, xg, xn, xl = (sb(f"x{i}", [C, L]) for i in "rgnl")
        FE = sb("FE", [112, 55, C])
        t0, t1_, t2_, t3_ = (sb(f"t{i}", [C, 2, T]) for i in range(4))
        S, R, E = sb("S", [112, 2, 2, T]), sb("R", [112, 2, 2, T]), sb("E", [112, 2, 2, T])
        WT = sb("WT", [112, 2, 8, 112])
        m8, nb, den = sb("m8", [112, 2, 8]), sb("nb", [112, 2]), sb("den", [112, 2, 2])
        hid = sb("hid", [C, 2, 2, T])
        yo = sb("yo", [C, 2, T])
        small = sb("small", [128, 8])
        ld = [P.dma(a[:], D[k]) for a, k in ((w1, "w1"), (b1, "b1"), (w2, "w2"), (b2, "b2"), (lg, "l2lg"),
                                             (lb, "l2lb"), (mask, "mask"))]
        for b in range(NI):
            lx = [P.dma(xres[:], src[b]), P.dma(xg[:], src[b])]
            gn = groupnorm(P, K, K["gn"][:], xg[:], 7, [lx, P.pe.last], xn[:], small)
            f0, f1, f2, f3 = ([None] * 9 for _ in range(4))
            v1, v2, v3 = {}, {}, {}

            def st0(t):
                s, cols = t % 2, slice(t * T, t * T + T)
                a = P.act(act(t0[:, s, :], xg[:, cols], ACT.Square), gn, f0[t - 2])
                f0[t] = P.pe(mm(PS[0:C, s, 0:T], K["ones"][0:C, 0:C], t0[:, s, :]), a, f1[t - 2])
                v1[t] = P.pe(mm(PS[0:C, 2 + s, 0:T], K["mean96"][0:C, 0:C], xg[:, cols]), gn, f2[t - 2])

            def st1(t):
                s, cols = t % 2, slice(t * T, t * T + T)
                f2[t] = P.dve(tt(xl[:, cols], xg[:, cols], PS[0:C, 2 + s, 0:T], ALU.subtract), v1[t])
                f1[t] = P.act(act(t1_[:, s, :], PS[0:C, s, 0:T], ACT.Sqrt), f0[t], v2.get(t - 2))
                a = P.act(act(t2_[:, s, :], xl[:, cols], ACT.Square), f2[t], v3.get(t - 2))
                v3[t] = P.pe(mm(PS[0:C, 4 + s, 0:T], K["mean96"][0:C, 0:C], t2_[:, s, :]), a, f3[t - 2])

            def st2(t):
                s, cols = t % 2, slice(t * T, t * T + T)
                f3[t] = P.act(act(t3_[:, s, :], PS[0:C, 4 + s, 0:T], ACT.Sqrt, bias=K["eps5"][0:C, :]), v3[t], v2.get(("x", t - 2)))
                a = P.dve(ts(t1_[:, s, :], t1_[:, s, :], 1e-12, None, ALU.max), f1[t])
                c_ = P.dve(lambda e, s=s: e.reciprocal(t3_[:, s, :], t3_[:, s, :]), f3[t])
                a = P.dve(lambda e, s=s: e.reciprocal(t1_[:, s, :], t1_[:, s, :]), a)
                c_ = P.dve(tt(xl[:, cols], xl[:, cols], t3_[:, s, :], ALU.mult), c_)
                v2["x", t] = c_
                v2[t] = P.dve(tt(xn[:, cols], xg[:, cols], t1_[:, s, :], ALU.mult), a)
                P.dve(ts(xl[:, cols], xl[:, cols], lg[:], lb[:], ALU.mult, ALU.add), c_, ld)

            for t in range(NT + 2):
                if t < NT:
                    st0(t)
                if 0 <= t - 1 < NT:
                    st1(t - 1)
                if t >= 2:
                    st2(t - 2)
            normed = P.dve.last
            free = [None, None]
            P.pe.wait(f1[NT - 1])
            for i in range(55):
                r0 = 2 * i if i < 28 else 2 * (i - 28) + 1
                s = 6 + i % 2
                a = P.pe(lambda e, s=s, r0=r0: e.transpose(PS[0:112, s, 0:C], xg[:, 56 * r0:56 * r0 + 112],
                                                            K["ident"][0:C, 0:C]), free[i % 2], gn)
                free[i % 2] = P.act(act(FE[:, i, :], PS[0:112, s, 0:C], ACT.Copy), a)
            P.pe.wait(normed, free)
            NQ = 28
            tk = {}

            flat = lambda b, s: b[:, s].rearrange("p a b -> p (a b)")
            start = lambda t: min(max(2 * t - 7, 0), 40)

            def sims(t):
                s, ks = t % 2, start(t)
                for i in range(2):
                    a = P.pe(mm(PS[0:112, 2 * s + i, 0:T], xn[:, 112 * t:112 * t + 112],
                                xn[:, ks * 56 + T * i:ks * 56 + T * i + T]), tk.get(("S", t - 2)))
                tk["P", t] = a

            def masked(t):
                s = t % 2
                mo = (start(t) - 2 * t + 14) * 56
                tk["S", t] = P.dve(tt(S[:, s], PS[0:112, 2 * s:2 * s + 2, 0:T],
                                      mask[:, mo:mo + 2 * T].rearrange("p (a b) -> p a b", b=T), ALU.add),
                                   tk["P", t], ld, tk.get(("E", t - 2)))

            def top(t):
                s = t % 2
                tk["m", t] = P.dve(lambda e: e.max(m8[:, s, :], flat(S, s)), tk["S", t])

            def negmax(t):
                s = t % 2
                a = P.dve(ts(nb[:, s:s + 1], m8[:, s, 0:1], -1.0, None, ALU.mult), tk["m", t])
                tk["R", t] = P.dve(lambda e: e.match_replace(flat(R, s), m8[:, s, :], flat(S, s), -3e9))
                tk["E", t] = P.act(act(flat(E, s), flat(S, s), ACT.Exp, bias=nb[:, s:s + 1]), a, tk.get(("T", t - 2)))

            def chosen(t):
                s = t % 2
                tk["W", t] = P.dve(stt(flat(E, s), flat(R, s), -2e9, flat(E, s), ALU.is_le, ALU.mult,
                                       accum_out=den[:, s, 0:1]), tk["E", t], tk["R", t])

            def divide(t):
                s = t % 2
                tk["r", t] = P.dve(lambda e: e.reciprocal(den[:, s, 1:2], den[:, s, 0:1]), tk["W", t])

            def scale_(t):
                s = t % 2
                tk["W", t] = P.dve(ts(flat(E, s), flat(E, s), den[:, s, 1:2], None, ALU.mult), tk["r", t])

            def turn(t):
                s = t % 2
                for i in range(8):
                    o = PS[0:112, 4 + i // 4, 112 * (i % 4):112 * (i % 4) + 112]
                    a = P.pe(lambda e, o=o, i=i: e.transpose(o, flat(E, s)[:, 112 * i:112 * i + 112],
                                                             K["ident"][0:112, 0:112]),
                             tk["W", t], tk.get(("F", i // 4)))
                    if i % 4 == 3:
                        h = i // 4
                        tk["F", h] = P.act(act(WT[:, s, 4 * h:4 * h + 4].rearrange("p b c -> p (b c)"),
                                               PS[0:112, 4 + h, 0:T], ACT.Copy), a, tk.get(("G", t - 2)))
                tk["T", t] = a
                tk["t", t] = tk["F", 1]

            def gathered(t):
                s, ks = t % 2, start(t)
                blk = ks // 2 if ks % 2 == 0 else 28 + (ks - 1) // 2
                for i in range(8):
                    a = P.pe(mm(PS[0:C, 6 + s, 0:112], FE[:, blk + i, :], WT[:, s, i, :], start=(i == 0), stop=(i == 7)),
                             tk["t", t], tk.get(("X", t - 2)))
                tk["G", t] = a

            def added(t):
                cols = slice(112 * t, 112 * t + 112)
                tk["X", t] = P.dve(tt(xl[:, cols], xl[:, cols], PS[0:C, 6 + t % 2, 0:112], ALU.add), tk["G", t])

            for r in range(NQ + 4):
                for fn, lag in ((sims, 0), (chosen, 2), (masked, 1), (divide, 2), (top, 1), (scale_, 2), (negmax, 1),
                                (turn, 2), (gathered, 3), (added, 4)):
                    if 0 <= r - lag < NQ:
                        fn(r - lag)
            P.pe.wait(P.dve.last)
            P.act.wait(P.pe.last)
            hfree, ofree, yf = [None] * 2, [None] * 2, [None] * 2
            for t in range(NT):
                s, cols = t % 2, slice(t * T, t * T + T)
                for i in range(2):
                    p = PS[0:C, 2 * s + i, 0:T]
                    a = P.pe(mm(p, w1[:, C * i:C * i + C], xl[:, cols]), ofree[s])
                    h = P.act(act(hid[:, s, i, :], p, ACT.Relu, bias=b1[:, i:i + 1]), a, hfree[s])
                p = PS[0:C, 4 + s, 0:T]
                for i in range(2):
                    a = P.pe(mm(p, w2[:, i, :], hid[:, s, i, :], start=(i == 0), stop=(i == 1)), h, ofree[s])
                hfree[s] = a
                a = P.dve(stt(yo[:, s, :], p, b2[:], xl[:, cols], ALU.add, ALU.add), a, yf[s])
                ofree[s] = a = P.dve(tt(yo[:, s, :], yo[:, s, :], xres[:, cols], ALU.add), a)
                yf[s] = P.dma(dst[b][:, cols], yo[:, s, :], a)
            P.barrier()
        P.barrier()


def program(nc, D, x, out, stages=(0, 1, 2, 3)):
    with ExitStack() as ctx:
        P = Program(nc, ctx)
        K = {}
        lds = []
        for name, shape in (("ident", [128, 128]), ("gn", [C, C]), ("blk", [128, 128]), ("mean96", [C, C])):
            K[name] = P.sb(ctx, name, shape)
            lds.append(P.dma(K[name][:], D[name]))
        K["sel"] = P.sb(ctx, "sel", [C, 16, 128], BF16)
        K["identb"] = P.sb(ctx, "identb", [128, 128], BF16)
        K["ones"] = P.sb(ctx, "ones", [128, 128])
        P.dve(lambda e: e.memset(K["ones"][:], 1.0))
        for name, v in (("eps5", 1e-5), ("one", 1.0), ("mone", -1.0), ("lneps", 13.815510557964274)):
            K[name] = P.sb(ctx, name, [128, 1])
            P.dve(lambda e, t=K[name], v=v: e.memset(t[:], v))
        P.dve(copy(K["identb"][:], K["ident"][:]), lds)
        with ExitStack() as c2:
            self_ = P.sb(c2, "self", [C, 16, 128])
            a = P.dma(self_[:], D["sel"])
            P.dve(copy(K["sel"][:], self_[:]), a)
            P.barrier()
        xd = x.rearrange("b c h w -> b c (h w)")
        od = out.rearrange("b c h w -> b c (h w)")
        zd = nc.dram_tensor("zscratch", (2, 128, 3, L), F32, kind="Internal").ap()
        mid = [nc.dram_tensor(f"mid{i}", (NI, C, L), F32, kind="Internal").ap() for i in range(3)]
        scr = [nc.dram_tensor(f"rows{i}", (1, L), F32, kind="Internal").ap() for i in range(4)]
        chain = [xd] + mid[:len(stages) - 1] + [od]
        for i, s in enumerate(stages):
            a, b = chain[i], chain[i + 1]
            if s == 0:
                attention(P, K, D, a, b, scr)
            elif s == 1:
                ssm(P, K, D, L1, a, b, zd)
            elif s == 2:
                local(P, K, D, a, b)
            else:
                ssm(P, K, D, L3, a, b, zd)
        P.emit()



def constants():
    g = {}
    g["ident"] = np.eye(128, dtype=np.float32)
    i = np.arange(C)
    g["gn"] = np.where(i[:, None] // 3 == i[None, :] // 3, 1.0 / (3 * L), 0.0).astype(np.float32)
    p = np.arange(128)
    g["blk"] = np.where(p[:, None] // 64 == p[None, :] // 64, 1.0 / 192, 0.0).astype(np.float32)
    g["mean96"] = np.full((C, C), 1.0 / 96, np.float32)
    sel = np.zeros((3, 2, 16, 16, 2, 64), np.float32)
    for n in range(16):
        for m in range(2):
            sel[:, m, n, n, m, :] = 1.0
    g["sel"] = sel.reshape(C, 16, 128)
    comb = np.zeros((4, 32, 32), np.float32)
    comb[:, np.arange(32), np.arange(32)] = 1.0
    g["comb"] = comb.reshape(128, 32)
    q = np.arange(112)
    qy, qx = q // 56, q % 56
    ry = np.arange(-14, 16)
    kx = np.arange(56)
    ok = (abs(ry[None, :, None] - qy[:, None, None]) <= 7) & (abs(kx[None, None, :] - qx[:, None, None]) <= 7)
    g["mask"] = np.where(ok, 0.0, -1e9).astype(np.float32).reshape(112, 30 * 56)
    return g


def paired(a):
    a = np.asarray(a).reshape((3, 64) + np.asarray(a).shape[1:])
    a = np.moveaxis(a, 0, 1)
    return np.ascontiguousarray(np.concatenate([a, a], axis=0))


def scan_weights(pre, g, xp, dw, db, A, ds):
    nk = xp.shape[0]
    o = np.zeros((nk, 2, 64, 3, 76), np.float32)
    for m in range(2):
        for c in range(3):
            blk = np.swapaxes(xp[:, :, 64 * c:64 * c + 64], 1, 2)
            o[:, m, :, c, 16 * m:16 * m + 16] = blk[:, :, 6:22]
            o[:, m, :, c, 32 + 16 * m:48 + 16 * m] = blk[:, :, 22:38]
            o[:, m, :, c, 64 + 6 * m:70 + 6 * m] = blk[:, :, 0:6]
    g[pre + "xp"] = o.reshape(nk, 128, 3, 76)
    d = np.zeros((nk, 2, 6, 3, 2, 64), np.float32)
    for m in range(2):
        d[:, m, :, :, m, :] = np.swapaxes(dw, 1, 2).reshape(nk, 6, 3, 64)
    g[pre + "dw"] = d.reshape(nk, 12, 3, 128)
    g[pre + "A"] = np.ascontiguousarray(np.swapaxes(paired(np.moveaxis(A.reshape(nk, 192, 16), 0, 1)), 1, 2))
    g[pre + "db"] = np.ascontiguousarray(np.swapaxes(paired(np.moveaxis(db.reshape(nk, 192), 0, 1)), 1, 2))
    g[pre + "ds"] = paired(np.moveaxis(ds.reshape(nk, 192), 0, 1))


def layout(v):
    g = constants()
    t = lambda a: np.ascontiguousarray(np.asarray(a).T)
    wq = np.asarray(v["L0_conv_w_qkv"])
    g["wqk"], g["wv"] = t(wq[0:96]), t(wq[96:144])
    g["wp"] = np.ascontiguousarray(np.moveaxis(t(v["L0_conv_w_proj"]).reshape(3, 16, C), 0, 1))
    g["bp"] = np.asarray(v["L0_conv_b_proj"]).reshape(C, 1)
    for pre, s, win in (("l1", "L1_conv_", "w_in"), ("l3", "L3_conv_", "in_proj_w")):
        g[pre + "win"] = t(v[s + win])
        g[pre + "cw"] = paired(np.asarray(v[s + "conv_w"]).reshape(192, 9))
        g[pre + "cb"] = paired(v[s + "conv_b"])
    f = lambda k: np.asarray(v[k])
    scan_weights("l1", g, f("L1_conv_x_proj_weight"), f("L1_conv_dt_projs_weight"), f("L1_conv_dt_projs_bias"),
                 f("L1_conv_A_logs"), f("L1_conv_Ds"))
    scan_weights("l3", g, f("L3_conv_x_proj_w"), f("L3_conv_dt_proj_w"), f("L3_conv_dt_proj_b"),
                 f("L3_conv_A_log"), f("L3_conv_Ds"))
    g["l1lg"], g["l1lb"], g["l1wo"] = paired(f("L1_conv_ln_w")), paired(f("L1_conv_ln_b")), paired(t(f("L1_conv_w_out")))
    g["w1"], g["b1"] = t(f("L2_conv_w1")), t(f("L2_conv_b1").reshape(2, C))
    g["w2"] = np.ascontiguousarray(np.moveaxis(t(f("L2_conv_w2")).reshape(2, C, C), 0, 1))
    g["b2"], g["l2lg"], g["l2lb"] = (f(k).reshape(C, 1) for k in ("L2_conv_b2", "L2_conv_ln_w", "L2_conv_ln_b"))
    g["l3lg"], g["l3lb"] = paired(f("L3_conv_ln_g")), paired(f("L3_conv_ln_b"))
    g["c1w"] = paired(t(f("L3_conv_c1_w").reshape(384, 192)))
    col = lambda a: np.ascontiguousarray(np.moveaxis(a.reshape((3, 128) + a.shape[1:]), 0, 1))
    g["c1b"], g["c2b"] = col(f("L3_conv_c1_b")), col(f("L3_conv_c2_b"))
    g["c2w"] = col(f("L3_conv_c2_w").reshape(384, 9))
    for i in "12":
        g["bn" + i] = np.ascontiguousarray(np.stack([col(f(f"L3_conv_bn{i}_{j}")) for j in "gbmv"], axis=1))
    g["c3w"] = col(t(f("L3_conv_c3_w").reshape(C, 384)))
    g["c3b"] = f("L3_conv_c3_b").reshape(C, 1)
    g["s1w"], g["s1b"] = t(f("L3_conv_se1_w")), f("L3_conv_se1_b").reshape(48, 1)
    g["s2w"], g["s2b"] = t(f("L3_conv_se2_w")), f("L3_conv_se2_b").reshape(C, 1)
    return g


def make(nc, v, stages=(0, 1, 2, 3)):
    arrays = {"x": np.ascontiguousarray(np.asarray(v["x"]))}
    arrays.update(layout(v))
    D = {n: nc.dram_tensor(f"in_{n}", a.shape, F32, kind="ExternalInput").ap() for n, a in arrays.items()}
    out = nc.dram_tensor("out_0", (NI, C, H, W), F32, kind="ExternalOutput").ap()
    program(nc, D, D.pop("x"), out, stages)
    return {f"in_{n}": a for n, a in arrays.items()}


def kernel(**inputs):
    import concourse.bacc as _bacc
    from concourse.bass_utils import run_bass_kernel_spmd as _run

    nc = _bacc.Bacc("TRN2", target_bir_lowering=False, num_devices=1)
    arrays = make(nc, inputs)
    r = _run(nc, [arrays], core_ids=[0])
    return r.results[0]["out_0"]
```
